# Optimizing a Trainium2 kernel written in Bass

```python
import numpy as np
import jax
import jax.numpy as jnp

def _softmax(x, axis=-1):
    return jax.nn.softmax(x, axis=axis)

def _gelu(x):
    return jax.nn.gelu(x, approximate=True)

def _silu(x):
    return jax.nn.silu(x)

def _sigmoid(x):
    return jax.nn.sigmoid(x)

def _layernorm(x, axis=-1, eps=1e-05):
    m = jnp.mean(x, axis=axis, keepdims=True)
    v = jnp.var(x, axis=axis, keepdims=True)
    return (x - m) / jnp.sqrt(v + eps)

def _scatter_add(tgt, idx, src, axis=0):
    return tgt.at[idx].add(src)

def _segment_sum(src, seg, n):
    return jax.ops.segment_sum(src, seg, n)
kernel_name = 'mk_adaln_ffn_d1_seqx_r4_790bca'

def setup_inputs(seed: int=0):
    np.random.seed(seed)
    _w = jnp.asarray

    def _rec_inputs():
        import jax
        import jax.numpy as jnp
        _rk = jax.random.key(seed)
        x = 7.22e-05 + 1 * jax.random.normal(jax.random.fold_in(_rk, 1), (8, 256, 512), jnp.float32)
        _lenS = 256 - jax.random.randint(jax.random.fold_in(_rk, 7), (8,), 0, max(1, 256 // 4) + 1, jnp.int32)
        _lenS2 = 256 - jax.random.randint(jax.random.fold_in(_rk, 8), (8,), 0, max(1, 256 // 4) + 1, jnp.int32)
        cond_2048 = jax.random.bernoulli(jax.random.fold_in(_rk, 11), 0.8975, (8, 512)).astype(jnp.float32)
        return (x, cond_2048)
    x, cond_2048 = _rec_inputs()

    def _L0_cond_setup():
        import jax, jax.numpy as jnp
        import numpy as np
        import math
        D_MODEL = 256
        NUM_HEAD = 16
        NEG_INF = -1e+30
        key = jax.random.key(seed)
        k_x, k_m, k_q, k_k, k_v = jax.random.split(key, 5)
        B, C, T = (4, D_MODEL, 512)
        x = jax.random.normal(k_x, (B, C, T), dtype=jnp.float32)
        mask = (jax.random.uniform(k_m, (B, T)) < 0.9).astype(jnp.float32)
        limit = math.sqrt(6.0 / (C + C))
        Wq = jax.random.uniform(k_q, (C, C), minval=-limit, maxval=limit, dtype=jnp.float32)
        Wk = jax.random.uniform(k_k, (C, C), minval=-limit, maxval=limit, dtype=jnp.float32)
        Wv = jax.random.uniform(k_v, (C, C), minval=-limit, maxval=limit, dtype=jnp.float32)
        b = jnp.zeros((1,), dtype=jnp.float32)
        return {'x': x, 'mask': mask, 'Wq': Wq, 'Wk': Wk, 'Wv': Wv, 'b': b}
    _L0_cond_all = _L0_cond_setup()
    _L0_cond_in = {k: v for k, v in _L0_cond_all.items() if k in ('Wq', 'Wk', 'Wv', 'b')}
    del _L0_cond_all

    def _L0_ffn_setup():
        import jax, jax.numpy as jnp
        import numpy as np
        BLOCK_SIZE = 32
        HIDDEN_SIZE = 512
        MLP_DIM = 4096
        NVFP4_LUT = jnp.array([0.0, 0.5, 1.0, 1.5, 2.0, 3.0, 4.0, 6.0, 0.0, -0.5, -1.0, -1.5, -2.0, -3.0, -4.0, -6.0], dtype=jnp.float32)

        def dequant_nvfp4(W_packed, scales, block=BLOCK_SIZE):
            N = W_packed.shape[0]
            low = W_packed & 15
            high = W_packed >> 4 & 15
            idx = jnp.stack([low, high], axis=-1).reshape(N, -1)
            vals = NVFP4_LUT[idx]
            K = vals.shape[1]
            vals = vals.reshape(N, K // block, block) * scales[:, :, None]
            return vals.reshape(N, K)
        key = jax.random.key(seed)
        ks = jax.random.split(key, 7)
        x = jax.random.normal(ks[0], (4, 32, HIDDEN_SIZE), dtype=jnp.float32)
        gate_W_packed = jax.random.randint(ks[1], (MLP_DIM, HIDDEN_SIZE // 2), 0, 64, dtype=jnp.int32)
        gate_scales = jax.random.uniform(ks[2], (MLP_DIM, HIDDEN_SIZE // BLOCK_SIZE), dtype=jnp.float32) * 0.1 + 0.001
        up_W_packed = jax.random.randint(ks[3], (MLP_DIM, HIDDEN_SIZE // 2), 0, 64, dtype=jnp.int32)
        up_scales = jax.random.uniform(ks[4], (MLP_DIM, HIDDEN_SIZE // BLOCK_SIZE), dtype=jnp.float32) * 0.1 + 0.001
        down_W_packed = jax.random.randint(ks[5], (HIDDEN_SIZE, MLP_DIM // 2), 0, 64, dtype=jnp.int32)
        down_scales = jax.random.uniform(ks[6], (HIDDEN_SIZE, MLP_DIM // BLOCK_SIZE), dtype=jnp.float32) * 0.1 + 0.001
        return {'x': x, 'gate_W_packed': gate_W_packed, 'gate_scales': gate_scales, 'up_W_packed': up_W_packed, 'up_scales': up_scales, 'down_W_packed': down_W_packed, 'down_scales': down_scales}
    _L0_ffn_all = _L0_ffn_setup()
    _L0_ffn_in = {k: v for k, v in _L0_ffn_all.items() if k in ('gate_W_packed', 'gate_scales', 'up_W_packed', 'up_scales', 'down_W_packed', 'down_scales')}
    del _L0_ffn_all
    return {'x': x, 'cond_2048': cond_2048, 'L0_cond_Wq': _L0_cond_in['Wq'], 'L0_cond_Wk': _L0_cond_in['Wk'], 'L0_cond_Wv': _L0_cond_in['Wv'], 'L0_cond_b': _L0_cond_in['b'], 'L0_ffn_gate_W_packed': _L0_ffn_in['gate_W_packed'], 'L0_ffn_gate_scales': _L0_ffn_in['gate_scales'], 'L0_ffn_up_W_packed': _L0_ffn_in['up_W_packed'], 'L0_ffn_up_scales': _L0_ffn_in['up_scales'], 'L0_ffn_down_W_packed': _L0_ffn_in['down_W_packed'], 'L0_ffn_down_scales': _L0_ffn_in['down_scales']}

def reference(x, cond_2048, L0_cond_Wq, L0_cond_Wk, L0_cond_Wv, L0_cond_b, L0_ffn_gate_W_packed, L0_ffn_gate_scales, L0_ffn_up_W_packed, L0_ffn_up_scales, L0_ffn_down_W_packed, L0_ffn_down_scales):
    import jax
    import jax.numpy as jnp

    def _L0_cond_ref(x, mask, Wq, Wk, Wv, b):
        import jax, jax.numpy as jnp
        import numpy as np
        import math
        D_MODEL = 256
        NUM_HEAD = 16
        NEG_INF = -1e+30
        B, C, T = x.shape
        H = NUM_HEAD
        Dh = C // H

        def proj(W):
            y = jnp.einsum('oc,bct->bto', W, x)
            return y.reshape(B, T, H, Dh).transpose(0, 2, 1, 3)
        Q, K, V = (proj(Wq), proj(Wk), proj(Wv))
        att = jnp.einsum('bhqd,bhkd->bhqk', Q, K) * (1.0 / math.sqrt(Dh))
        att = att + b[0]
        m = mask[:, None, None, :]
        att = att * m + (1.0 - m) * NEG_INF
        att = jax.nn.softmax(att, axis=-1)
        y = jnp.einsum('bhqk,bhkd->bhqd', att, V)
        y = y.transpose(0, 2, 1, 3).reshape(B, T, C)
        return y.transpose(0, 2, 1)

    def _L0_ffn_ref(x, gate_W_packed, gate_scales, up_W_packed, up_scales, down_W_packed, down_scales):
        import jax, jax.numpy as jnp
        import numpy as np
        BLOCK_SIZE = 32
        HIDDEN_SIZE = 512
        MLP_DIM = 4096
        NVFP4_LUT = jnp.array([0.0, 0.5, 1.0, 1.5, 2.0, 3.0, 4.0, 6.0, 0.0, -0.5, -1.0, -1.5, -2.0, -3.0, -4.0, -6.0], dtype=jnp.float32)

        def dequant_nvfp4(W_packed, scales, block=BLOCK_SIZE):
            N = W_packed.shape[0]
            low = W_packed & 15
            high = W_packed >> 4 & 15
            idx = jnp.stack([low, high], axis=-1).reshape(N, -1)
            vals = NVFP4_LUT[idx]
            K = vals.shape[1]
            vals = vals.reshape(N, K // block, block) * scales[:, :, None]
            return vals.reshape(N, K)
        B, S, H = x.shape
        xt = x.reshape(B * S, H)
        Wg = dequant_nvfp4(gate_W_packed, gate_scales)
        Wu = dequant_nvfp4(up_W_packed, up_scales)
        Wd = dequant_nvfp4(down_W_packed, down_scales)
        gate = jnp.einsum('th,nh->tn', xt, Wg)
        up = jnp.einsum('th,nh->tn', xt, Wu)
        gelu = jnp.tanh(0.7978845608028654 * (gate + 0.044715 * gate ** 3)) * gate * 0.5 + gate * 0.5
        inter = gelu * up
        out = jnp.einsum('tn,hn->th', inter, Wd)
        return out.reshape(B, S, H)
    x = x + _L0_ffn_ref(_L0_cond_ref(x, cond_2048, L0_cond_Wq, L0_cond_Wk, L0_cond_Wv, L0_cond_b), L0_ffn_gate_W_packed, L0_ffn_gate_scales, L0_ffn_up_W_packed, L0_ffn_up_scales, L0_ffn_down_W_packed, L0_ffn_down_scales)
    return x

_drawn_inputs = setup_inputs


def setup_inputs(seed=0):
    import zlib

    import numpy as np

    out = dict(_drawn_inputs(seed))
    spreads = {}
    factors = {}
    for name, (base, spread) in spreads.items():
        noise = np.random.default_rng([zlib.crc32(name.encode()), seed]).standard_normal(out[name].shape)
        drawn = base * np.exp(spread * noise) if base else spread * noise
        out[name] = jnp.asarray(drawn.astype(out[name].dtype))
    for name, factor in factors.items():
        out[name] = (out[name] * factor).astype(out[name].dtype)
    return out
```

```python
from contextlib import ExitStack

import concourse.bass as bass
from concourse import mybir

P = 128
B, C, T = 8, 256, 512
F = 4096
NHEAD, DH = 16, 16
CK = C // P
TT = T // P
BLOCK = 32
QUADS = NHEAD // 4
UNIT_HEADS = P // DH

SEED_ROW = 64
MAX_ROW = 96
STACK_ROWS = 98
SEED_Q = 1024.0
MASK_K = 32768.0
MAX_K = 16.0
SCORE_SCALE = DH ** -0.5

Y_SCALE = 64.0
W_SCALE = 64.0
I_SCALE = 64.0
CODE_SCALE = 2.0 ** 14

GROUPS = 4
UNITS = F // P // GROUPS
CHUNKS = B * C // 512
WORDS = 2 * P + 2 * P + 256
DQ_STEPS = 5
STACK_DMAS = 9


def build(nc, x, mask, bias, wq, wk, wv, packed, scales, out):
    f32, f16, u32 = mybir.dt.float32, mybir.dt.float16, mybir.dt.uint32
    ALU, ACT, AX = mybir.AluOpType, mybir.ActivationFunctionType, mybir.AxisListType
    ctx = ExitStack()
    with ctx:
        def sb(name, shape, dt):
            return ctx.enter_context(nc.sbuf_tensor(name, shape, dt))

        def ps(name, shape, dt):
            return ctx.enter_context(nc.psum_tensor(name, shape, dt))

        def sem(name):
            return ctx.enter_context(nc.semaphore(name))

        y_hi = sb("y_hi", [P, TT, B * C], f16)
        y_lo = sb("y_lo", [P, TT, B * C], f16)
        w_even = [sb("w_even_hi", [P, UNITS, 2, WORDS], f16), sb("w_even_lo", [P, UNITS, 2, WORDS], f16)]
        dq_packed = sb("dq_packed", [P, WORDS], u32)
        dq_scales = sb("dq_scales", [P, WORDS], f32)
        dq_code = sb("dq_code", [P, WORDS], u32)
        dq_sign = sb("dq_sign", [P, WORDS], u32)
        dq_mag = sb("dq_mag", [P, WORDS], u32)
        dq_w = sb("dq_w", [P, 2, WORDS], f32)

        big = sb("big", [P, 8192], f32)
        p_exp = big[:, :].rearrange("p (a h k q) -> p a h k q", a=2, h=4, k=2)
        acc = big[:, :].rearrange("p (r h) -> p r h", h=T)
        wide = sb("wide", [P, 2 * UNITS * 2 * WORDS], f16)
        half = UNITS * 2 * WORDS
        w_odd = [wide[:, i * half:(i + 1) * half].rearrange("p (u e w) -> p u e w", u=UNITS, e=2) for i in range(2)]
        stack = NHEAD * T
        q_stack = wide[:, 0:stack].rearrange("p (h q) -> p h q", q=T)
        k_stack = wide[:, stack:2 * stack].rearrange("p (h q) -> p h q", q=T)
        v_words = TT * NHEAD * 32
        v_rows = wide[:, 2 * stack:2 * stack + 2 * v_words].bitcast(f32).rearrange(
            "p (k h d) -> p k h d", k=TT, h=NHEAD)
        parts = wide[:, 2 * stack + 2 * v_words:].rearrange("p (u n q) -> p u n q", u=2, q=T)
        qk = [[[parts[:, u, 2 * s + i, :] for i in range(2)] for u in range(2)] for s in range(2)]
        weights = [w_even, w_odd]

        small = sb("small", [P, 2560], f32)
        x_in = small[:, 0:1024].rearrange("p (k t) -> p k t", k=CK)
        w_proj = [small[:, 1024 + i * 512:1024 + (i + 1) * 512].rearrange("p (k o) -> p k o", k=CK) for i in range(3)]
        gelu = small[:, 0:1024].rearrange("p (i t) -> p i t", i=2)
        inter = small[:, 1024:2048].rearrange("p (i t) -> p i t", i=2)

        av_sb = sb("av_sb", [P, T], f32)
        y_f = sb("y_f", [P, TT, 64], f32)
        y_rec = sb("y_rec", [P, TT, 4], f32)
        maxima = sb("maxima", [P, 16], f32)
        max_rows = [sb("max_hi", [16, P], f16), sb("max_lo", [16, P], f16)]
        ident = sb("ident", [P, P], f32)
        any_key = sb("any_key", [P, B], f32)
        any_now = sb("any_now", [P, 1], f32)
        in_hi = sb("in_hi", [P, 2, T], f16)
        in_lo = sb("in_lo", [P, 2, T], f16)

        mask_all = big[:, 0:B * T]
        mask_b = big[0:B, 4096:4608]
        mask_s = big[0:B, 4608:5120]
        any_b = big[0:B, 5120:5121]
        bias_b = big[0:B, 5121:5122]
        bias_s = big[0:B, 5122:5123]
        bias_hi = big[0:B, 5124:5125].bitcast(f16)[:, 0:1]
        bias_lo = big[0:B, 5125:5126]
        seed = big[0:B, 5632:5632 + 768].bitcast(f16).rearrange("b (r t) -> b r t", r=3)
        seed_dram = nc.dram_tensor("seed_rows", [B, 3, T], f16, kind="Internal").ap()

        qk_dram = nc.dram_tensor("qk_parts", [2, 4, P, T], f16, kind="Internal").ap()

        psum = ps("psum", [P, 8, 512], f32)
        p_score, p_max, p_av, p_misc = psum[:, 0:4, :], psum[:, 4:6, :], psum[:, 6, :], psum[:, 7, :]
        p_gate, p_up, p_out = [psum[:, 0, :], psum[:, 2, :]], [psum[:, 1, :], psum[:, 3, :]], psum[:, 4:8, :]

        consts_in = sem("consts_in")
        ident_in = sem("ident_in")
        setup = sem("setup")
        dve_own = sem("dve_own")
        any_set = sem("any_set")
        seed_out = sem("seed_out")
        x_loaded = sem("x_loaded")
        qk_proj = sem("qk_proj")
        qk_hi = sem("qk_hi")
        qk_lo = sem("qk_lo")
        v_proj = sem("v_proj")
        v_ready = sem("v_ready")
        qk_out = [sem("qk_out0"), sem("qk_out1")]
        stack_in = [sem("stack_in0"), sem("stack_in1")]
        max_mm = sem("max_mm")
        max_red = sem("max_red")
        max_t = sem("max_t")
        max_hi_s = sem("max_hi_s")
        max_lo_s = sem("max_lo_s")
        max_in = sem("max_in")
        score_mm = sem("score_mm")
        exp_done = sem("exp_done")
        av_done = sem("av_done")
        av_out = sem("av_out")
        y_t = sem("y_t")
        y_rec_s = sem("y_rec_s")
        y_norm = sem("y_norm")
        y_hi_s = sem("y_hi_s")
        y_lo_s = sem("y_lo_s")
        dq_in = sem("dq_in")
        dq_step = sem("dq_step")
        w_hi_s = sem("w_hi_s")
        w_lo_s = sem("w_lo_s")
        acc_in = sem("acc_in")
        gate_mm = sem("gate_mm")
        up_mm = sem("up_mm")
        gelu_s = sem("gelu_s")
        inter_s = sem("inter_s")
        in_hi_s = sem("in_hi_s")
        in_lo_s = sem("in_lo_s")
        down_mm = sem("down_mm")
        sum_mm = sem("sum_mm")
        acc_add = sem("acc_add")
        stored = sem("stored")

        act_spare = nc.scalar.alloc_register("act_spare")
        pool_spare = nc.gpsimd.alloc_register("pool_spare")
        block = ctx.enter_context(nc.Block())

        PLAN = [
            ["S0a", "M3", "AVb", "S1a", "M3", "S2a", "M3", "Y", "S3a", "M3", "S0b", "M2", "AVa", "S1b", "M2",
             *extra, "S2b", "MT", *late, "S3b"]
            for extra, late in ((["V1"], []), ([], ["Q0", "K0"]), ([], []), (["Q1"], ["K1", "V0"]))
        ]

        def plan(g, first, last):
            for step in PLAN[g]:
                if first and g == 0 and step in ("AVb", "Y"):
                    continue
                if last and (step in ("Q0", "K0", "Q1", "K1", "V0") or (g == 3 and (step[0] == "M"))):
                    continue
                yield step

        def batches(eng, body):
            body(0, True, False)
            with eng.Fori(1, B - 1) as b:
                body(b, False, False)
            body(B - 1, False, True)

        def first_steps(s, count):
            return isinstance(s, int) and s < count

        def chunks(eng, body):
            for g in range(GROUPS):
                if g == 0:
                    body(0, 0)
                with eng.Fori(1 if g == 0 else 0, CHUNKS) as t:
                    body(g, t)

        def wait_apart(eng, spare, sem, value):
            eng.wait_ge(sem, value)
            eng.reg_mov(spare, 0)

        def unit_of(w, u):
            return w[:, u] if isinstance(u, int) else w[:, bass.ds(u, 1)].rearrange("p u e w -> p (u e) w")

        def load_x(sp, b):
            sp.dma_start(x_in, x[b].rearrange("(k p) t -> p k t", p=P)).then_inc(x_loaded, 16)

        def load_unit(sp, n, count):
            if not (isinstance(count, int) and count == 0):
                sp.wait_ge(dq_step, DQ_STEPS * count)
            sp.dma_start(dq_packed[:, :], packed[n]).then_inc(dq_in, 16)
            sp.dma_start(dq_scales[:, :], scales[n].unsqueeze(1).broadcast_to([8, 16, WORDS])).then_inc(dq_in, 16)

        def store_qk(sp, b, u):
            sp.wait_ge(qk_lo, 4 * b + 2 * u + 2)
            sp.dma_start(qk_dram[u].rearrange("n p q -> p n q"), parts[:, u]).then_inc(qk_out[u], 16)

        def fill_stack(sp, b, u, first):
            sp.wait_ge(qk_out[u], 16 * b + 16)
            if not first:
                sp.wait_ge(score_mm, 32 * (b - 1) + 16 * u + 16)
            heads = slice(u * UNIT_HEADS, (u + 1) * UNIT_HEADS)
            for side, (dst, order) in enumerate(((q_stack, (0, 0, 1, 1)), (k_stack, (0, 1, 0, 1)))):
                for j, i in enumerate(order):
                    sp.dma_start(dst[j * DH:(j + 1) * DH, heads, :],
                                 qk_dram[u, 2 * side + i].rearrange("(h r) q -> r h q", r=DH)).then_inc(stack_in[u], 16)
            sp.dma_start(k_stack[SEED_ROW:SEED_ROW + 3, heads, :],
                         seed_dram[b].unsqueeze(1).broadcast_to([3, UNIT_HEADS, T])).then_inc(stack_in[u], 16)

        def move_max(sp, b, g):
            sp.wait_ge(max_lo_s, 4 * b + g + 1)
            for i in range(2):
                sp.dma_start(q_stack[MAX_ROW + i:MAX_ROW + i + 1, 4 * g:4 * g + 4, :].rearrange(
                    "o h (t q) -> o (h t) q", q=P), max_rows[i][:, :]).then_inc(max_in, 16)

        def weight_lo(pool, n, w, u):
            wait_apart(pool, pool_spare, w_hi_s, n + 1)
            nc.gpsimd.tensor_tensor(unit_of(w[1], u), dq_w[:, :, :], unit_of(w[0], u),
                                    ALU.subtract).then_inc(w_lo_s, 1)

        def weight_hi(act, n, w, u):
            wait_apart(act, act_spare, dq_step, DQ_STEPS * n + DQ_STEPS)
            nc.scalar.copy(unit_of(w[0], u), dq_w[:, :, :]).then_inc(w_hi_s, 1)

        def decode(dve, n, k):
            done = DQ_STEPS * n
            if k == 0:
                dve.wait_ge(dq_in, 32 * n + 32)
                if not (isinstance(n, int) and n == 0):
                    dve.wait_ge(dq_step, done)
                nc.vector.scalar_tensor_tensor(out=dq_code[:, :], in0=dq_packed[:, :], scalar=12, in1=dq_packed[:, :],
                                               op0=ALU.logical_shift_left, op1=ALU.bitwise_or).then_inc(dq_step, 1)
            elif k == 1:
                dve.wait_ge(dq_step, done + 1)
                nc.vector.tensor_scalar(dq_sign[:, :], dq_code[:, :], 12, 0x80008000, ALU.logical_shift_left,
                                        ALU.bitwise_and).then_inc(dq_step, 1)
            elif k == 2:
                nc.vector.tensor_scalar(dq_mag[:, :], dq_code[:, :], 9, 0x0E000E00, ALU.logical_shift_left,
                                        ALU.bitwise_and).then_inc(dq_step, 1)
            elif k == 3:
                dve.wait_ge(dq_step, done + 3)
                nc.vector.tensor_tensor(dq_code[:, :], dq_sign[:, :], dq_mag[:, :],
                                        ALU.bitwise_or).then_inc(dq_step, 1)
            else:
                dve.wait_ge(dq_step, done + 4)
                if not (isinstance(n, int) and n == 0):
                    dve.wait_ge(w_lo_s, n)
                nc.vector.scalar_tensor_tensor(
                    out=dq_w[:, :, :], in0=dq_code[:, :].bitcast(f16).rearrange("p (w e) -> p e w", e=2),
                    scalar=CODE_SCALE * W_SCALE, in1=dq_scales[:, :].unsqueeze(1).broadcast_to([P, 2, WORDS]),
                    op0=ALU.mult, op1=ALU.mult).then_inc(dq_step, 1)

        @block.sync
        def _(sp):
            for i, w in enumerate((wq, wk, wv)):
                sp.dma_start(w_proj[i], w.rearrange("(k p) o -> p k o", p=P)).then_inc(consts_in, 16)
            load_x(sp, 0)
            sp.dma_start(mask_all, mask.rearrange("b t -> (b t)").partition_broadcast(P)).then_inc(consts_in, 16)
            sp.dma_start(mask_b, mask).then_inc(consts_in, 16)
            sp.dma_start(bias_b, bias.partition_broadcast(B)).then_inc(consts_in, 16)
            load_unit(sp, 0, 0)
            sp.wait_ge(setup, 8)
            sp.dma_start(seed_dram, seed).then_inc(seed_out, 16)
            sp.wait_ge(seed_out, 16)
            store_qk(sp, 0, 0)
            store_qk(sp, 0, 1)
            fill_stack(sp, 0, 0, True)
            move_max(sp, 0, 0)

            def body(b, first, last):
                fill_stack(sp, b, 1, first)
                if not last:
                    sp.wait_ge(v_proj, 2 * b + 2)
                    load_x(sp, b + 1)
                move_max(sp, b, 1)
                move_max(sp, b, 2)
                if not last:
                    store_qk(sp, b + 1, 0)
                    fill_stack(sp, b + 1, 0, False)
                move_max(sp, b, 3)
                load_unit(sp, b + 1, b + 1)
                if not last:
                    store_qk(sp, b + 1, 1)
                    move_max(sp, b + 1, 0)

            batches(sp, body)

            sp.wait_ge(av_done, 8 * B)
            for r in range(CHUNKS):
                sp.dma_start(acc[:, 4 * r:4 * r + 4, :],
                             x.rearrange("b (k p) t -> p (b k) t", p=P)[:, 4 * r:4 * r + 4, :]).then_inc(acc_in, 16)
            with sp.Fori(UNITS + 1, GROUPS * UNITS) as n:
                load_unit(sp, n, n)
            for t in range(CHUNKS):
                sp.wait_ge(acc_add, 4 * ((GROUPS - 1) * CHUNKS + t + 1))
                sp.dma_start(out[t * 512:(t + 1) * 512, :].rearrange("(r p) h -> p r h", p=P),
                             acc[:, 4 * t:4 * t + 4, :]).then_inc(stored, 16)
            sp.wait_ge(stored, 16 * CHUNKS)

        @block.gpsimd
        def _(pool):
            nc.gpsimd.memset(ident[:, :], 0.0).then_inc(ident_in, 1)
            pool.wait_ge(ident_in, 1)
            nc.gpsimd.affine_select(out=ident[:, :], in_=ident[:, :], compare_op=ALU.not_equal, fill=1.0, base=0,
                                    pattern=[[-1, P]], channel_multiplier=1).then_inc(ident_in, 1)

            def split_y(b, g):
                q = 4 * b + g
                cols = bass.ds(b * C + g * 64, 64)
                wait_apart(pool, pool_spare, y_norm, q + 1)
                nc.gpsimd.tensor_copy(y_hi[:, :, cols], y_f[:, :, :]).then_inc(y_hi_s, 1)
                wait_apart(pool, pool_spare, y_hi_s, q + 1)
                nc.gpsimd.tensor_tensor(y_lo[:, :, cols], y_f[:, :, :], y_hi[:, :, cols],
                                        ALU.subtract).then_inc(y_lo_s, 1)

            def body(b, first, last):
                if not first:
                    split_y(b - 1, 3)
                for g in range(3):
                    split_y(b, g)
                weight_lo(pool, b, weights[0], b)

            batches(pool, body)
            split_y(B - 1, 3)

            for g in range(GROUPS - 1):
                with pool.Fori(0, CHUNKS) as t:
                    for i in range(2):
                        weight_lo(pool, (g + 1) * UNITS + 2 * t + i, weights[(g + 1) % 2], 2 * t + i)

        @block.scalar
        def _(act):
            def qk_part(b, side, u, first):
                n = 4 * b + 2 * u + side
                if not first:
                    act.wait_ge(qk_out[u], 16 * b)
                    if side == 0 and u == 0:
                        act.wait_ge(any_set, b + 1)
                act.wait_ge(qk_proj, n + 1)
                scale = 1.0 if side else any_now[:, :]
                nc.scalar.activation(qk[side][u][0], p_misc, ACT.Copy, scale=scale).then_inc(qk_hi, 1)

            def v_part(b, u, first):
                act.wait_ge(v_proj, 2 * b + u + 1)
                if not first:
                    act.wait_ge(av_done, 8 * (b - 1) + 4 * u + 4)
                nc.scalar.activation(v_rows[:, :, u * UNIT_HEADS:(u + 1) * UNIT_HEADS, 0:DH],
                                     p_misc.rearrange("p (k h d) -> p k h d", k=TT, h=UNIT_HEADS),
                                     ACT.Copy).then_inc(v_ready, 1)

            def max_part(b, g, first):
                q = 4 * b + g
                act.wait_ge(max_t, q + 1)
                if not (first and g == 0):
                    act.wait_ge(max_in, 32 * q)
                nc.scalar.activation(max_rows[0][:, :], p_misc[0:16, 0:P], ACT.Copy,
                                     scale=-1.0 / MAX_K).then_inc(max_hi_s, 1)

            act.wait_ge(setup, 8)
            act.wait_ge(any_set, 1)
            qk_part(0, 0, 0, True)
            qk_part(0, 1, 0, True)
            qk_part(0, 0, 1, True)
            qk_part(0, 1, 1, True)
            v_part(0, 0, True)
            max_part(0, 0, True)

            def body(b, first, last):
                for g in range(QUADS):
                    q = 4 * b + g
                    for step in plan(g, first, last):
                        if step[0] == "S":
                            h, a = int(step[1]), "ab".index(step[2])
                            n = 8 * q + 4 * a + h
                            act.wait_ge(score_mm, n + 1)
                            if not (first and g == 0):
                                act.wait_ge(av_done, 2 * q - 1 + a)
                            nc.scalar.activation(p_exp[:, a, h], p_score[:, 2 * (h % 2):2 * (h % 2) + 2, :], ACT.Exp,
                                                 scale=SCORE_SCALE).then_inc(exp_done, 1)
                        elif step == "AVb":
                            copy_av(q - 1, first and g == 1)
                        elif step == "MT":
                            nb, ng = (b, g + 1) if g < 3 else (b + 1, 0)
                            max_part(nb, ng, False)
                        elif step == "V1":
                            v_part(b, 1, first)
                        elif step == "V0":
                            v_part(b + 1, 0, False)
                        elif step in ("Q0", "K0", "Q1", "K1"):
                            qk_part(b + 1, "QK".index(step[0]), int(step[1]), False)
                weight_hi(act, b, weights[0], b)

            def copy_av(q, first):
                act.wait_ge(av_done, 2 * q + 2)
                if not first:
                    act.wait_ge(y_t, q)
                nc.scalar.copy(av_sb[:, :], p_av).then_inc(av_out, 1)

            batches(act, body)
            copy_av(4 * B - 1, False)

            def chunk(g, t):
                for i in range(UNITS):
                    s = (g * CHUNKS + t) * UNITS + i
                    act.wait_ge(gate_mm, s + 1)
                    if not first_steps(s, 2):
                        act.wait_ge(inter_s, s - 1)
                    nc.scalar.activation(gelu[:, i % 2, :], p_gate[i % 2], ACT.Gelu_apprx_tanh,
                                         scale=1.0 / (Y_SCALE * W_SCALE)).then_inc(gelu_s, 1)
                    act.wait_ge(inter_s, s + 1)
                    c = g * CHUNKS + t
                    if i >= 2:
                        act.wait_ge(down_mm, (UNITS - 1) * c + i - 1)
                    elif not first_steps(s, 2):
                        if i == 0:
                            act.wait_ge(down_mm, (UNITS - 1) * c)
                        else:
                            act.wait_ge(sum_mm, 4 * c)
                    nc.scalar.copy(in_hi[:, i % 2, :], inter[:, i % 2, :]).then_inc(in_hi_s, 1)
                    if g < GROUPS - 1 and i % 4 == 3:
                        u = 2 * t + i // 4
                        weight_hi(act, (g + 1) * UNITS + u, weights[(g + 1) % 2], u)

            chunks(act, chunk)

        @block.vector
        def _(dve):
            nc.vector.memset(q_stack[SEED_ROW:MAX_ROW, :, :], SEED_Q).then_inc(setup, 1)
            nc.vector.memset(k_stack[SEED_ROW:MAX_ROW, :, :], 0.0).then_inc(setup, 1)
            nc.vector.memset(k_stack[MAX_ROW:STACK_ROWS, :, :], MAX_K).then_inc(setup, 1)
            nc.vector.memset(v_rows[:, :, :, :], 0.0).then_inc(setup, 1)
            dve.wait_ge(setup, 4)
            nc.vector.memset(v_rows[:, :, :, DH:DH + 1], 1.0 / Y_SCALE).then_inc(setup, 1)
            dve.wait_ge(consts_in, 96)
            nc.vector.reduce_max(any_key[:, :], mask_all.rearrange("p (b t) -> p b t", b=B), AX.X).then_inc(setup, 1)
            nc.vector.reduce_max(any_b, mask_b, AX.X).then_inc(dve_own, 1)
            nc.vector.tensor_scalar(mask_s, mask_b, 1.0, MASK_K, ALU.subtract, ALU.mult).then_inc(dve_own, 1)
            nc.vector.tensor_scalar(bias_s, bias_b, 1.0 / (SCORE_SCALE * SEED_Q), None, ALU.mult).then_inc(dve_own, 1)
            dve.wait_ge(dve_own, 3)
            nc.vector.tensor_scalar(seed[:, 0, :], mask_s, any_b, None, ALU.mult).then_inc(dve_own, 1)
            nc.vector.tensor_scalar(bias_s, bias_s, any_b, None, ALU.mult).then_inc(dve_own, 1)
            dve.wait_ge(dve_own, 5)
            nc.vector.tensor_copy(bias_hi, bias_s).then_inc(dve_own, 1)
            dve.wait_ge(dve_own, 6)
            nc.vector.tensor_tensor(bias_lo, bias_s, bias_hi, ALU.subtract).then_inc(dve_own, 1)
            nc.vector.tensor_scalar(mask_s, mask_b, 0.0, None, ALU.mult).then_inc(dve_own, 1)
            dve.wait_ge(dve_own, 8)
            nc.vector.tensor_scalar(seed[:, 1, :], mask_s, bias_hi, None, ALU.add).then_inc(setup, 1)
            nc.vector.tensor_scalar(seed[:, 2, :], mask_s, bias_lo, None, ALU.add).then_inc(setup, 1)

            def qk_part(b, side, u):
                n = 4 * b + 2 * u + side
                dve.wait_ge(qk_hi, n + 1)
                scale = 1.0 if side else any_now[:, :]
                nc.vector.scalar_tensor_tensor(out=qk[side][u][1], in0=p_misc, scalar=scale, in1=qk[side][u][0],
                                               op0=ALU.mult, op1=ALU.subtract).then_inc(qk_lo, 1)

            def reduce_maxima(b, g, n0, count, first):
                q = 4 * b + g
                if n0 == 0 and not first:
                    dve.wait_ge(max_t, q)
                for n in range(n0, n0 + count):
                    dve.wait_ge(max_mm, 16 * q + n + 1)
                    nc.vector.reduce_max(maxima[:, n:n + 1], p_max[:, n % 2, :], AX.X).then_inc(max_red, 1)

            def max_part(b, g):
                q = 4 * b + g
                dve.wait_ge(max_hi_s, q + 1)
                nc.vector.scalar_tensor_tensor(out=max_rows[1][:, :], in0=p_misc[0:16, 0:P], scalar=-1.0 / MAX_K,
                                               in1=max_rows[0][:, :], op0=ALU.mult,
                                               op1=ALU.subtract).then_inc(max_lo_s, 1)

            def normalise(q, first):
                rows = p_misc.rearrange("p (k h d) -> p k h d", k=TT, h=4)
                dve.wait_ge(y_t, q + 1)
                nc.vector.reciprocal(y_rec[:, :, :], rows[:, :, :, DH]).then_inc(y_rec_s, 1)
                dve.wait_ge(y_rec_s, q + 1)
                if not first:
                    dve.wait_ge(y_lo_s, q)
                nc.vector.tensor_tensor(y_f[:, :, :].rearrange("p k (h d) -> p k h d", h=4), rows[:, :, :, 0:DH],
                                        y_rec[:, :, :].unsqueeze(3).broadcast_to([P, TT, 4, DH]),
                                        ALU.mult).then_inc(y_norm, 1)

            dve.wait_ge(setup, 8)
            nc.vector.tensor_copy(any_now[:, :], any_key[:, 0:1]).then_inc(any_set, 1)
            for side, u in ((0, 0), (1, 0), (0, 1), (1, 1)):
                qk_part(0, side, u)
            reduce_maxima(0, 0, 0, 16, True)
            max_part(0, 0)

            def body(b, first, last):
                if not last:
                    nc.vector.tensor_copy(any_now[:, :], any_key[:, bass.ds(b + 1, 1)]).then_inc(any_set, 1)
                for g in range(QUADS):
                    q = 4 * b + g
                    nb, ng = (b, g + 1) if g < 3 else (b + 1, 0)
                    n = 0
                    for step in plan(g, first, last):
                        if step in ("M2", "M3"):
                            count = int(step[1])
                            reduce_maxima(nb, ng, n, count, False)
                            n += count
                        elif step == "MT":
                            max_part(nb, ng)
                        elif step == "Y":
                            normalise(q - 1, first and g == 1)
                        elif step in ("Q0", "K0", "Q1", "K1"):
                            qk_part(b + 1, "QK".index(step[0]), int(step[1]))
                    for k in ((0, 1, 2), (3,), (4,), ())[g]:
                        decode(dve, b, k)

            batches(dve, body)
            normalise(4 * B - 1, False)

            def chunk(g, t):
                for i in range(UNITS):
                    s = (g * CHUNKS + t) * UNITS + i
                    dve.wait_ge(gelu_s, s + 1)
                    dve.wait_ge(up_mm, s + 1)
                    if not first_steps(s, 2):
                        dve.wait_ge(in_lo_s, s - 1)
                    nc.vector.scalar_tensor_tensor(out=inter[:, i % 2, :], in0=p_up[i % 2],
                                                   scalar=I_SCALE / (Y_SCALE * W_SCALE), in1=gelu[:, i % 2, :],
                                                   op0=ALU.mult, op1=ALU.mult).then_inc(inter_s, 1)
                    dve.wait_ge(in_hi_s, s + 1)
                    nc.vector.tensor_tensor(in_lo[:, i % 2, :], inter[:, i % 2, :], in_hi[:, i % 2, :],
                                            ALU.subtract).then_inc(in_lo_s, 1)
                    if g < GROUPS - 1:
                        for k in ((0,), (1, 2), (3, 4), ())[i % 4]:
                            decode(dve, (g + 1) * UNITS + 2 * t + i // 4, k)
                c = g * CHUNKS + t
                for r in range(4):
                    dve.wait_ge(sum_mm, 4 * c + r + 1)
                    if g == 0:
                        dve.wait_ge(acc_in, 16 * CHUNKS)
                    rows = acc[:, bass.ds(4 * t + r, 1), :].rearrange("p r h -> p (r h)")
                    if not first_steps(c, 1) and g > 0:
                        dve.wait_ge(acc_add, 4 * (c - CHUNKS) + r + 1)
                    nc.vector.scalar_tensor_tensor(out=rows, in0=p_out[:, r, :], scalar=1.0 / (I_SCALE * W_SCALE),
                                                   in1=rows, op0=ALU.mult, op1=ALU.add).then_inc(acc_add, 1)

            chunks(dve, chunk)

        @block.tensor
        def _(pe):
            def project_qk(b, side, u):
                if side == 0 and u == 0:
                    pe.wait_ge(x_loaded, 16 * b + 16)
                for k in range(CK):
                    last = nc.tensor.matmul(p_misc, w_proj[side][:, k, u * P:(u + 1) * P], x_in[:, k, :],
                                            start=(k == 0), stop=(k == CK - 1))
                last.then_inc(qk_proj, 1)

            def project_v(b, u):
                for t in range(TT):
                    for k in range(CK):
                        last = nc.tensor.matmul(p_misc[:, t * P:(t + 1) * P], x_in[:, k, t * P:(t + 1) * P],
                                                w_proj[2][:, k, u * P:(u + 1) * P], start=(k == 0), stop=(k == CK - 1))
                last.then_inc(v_proj, 1)

            def max_tiles(b, g, n0, count, first):
                q = 4 * b + g
                if n0 == 0:
                    pe.wait_ge(stack_in[g // 2], 16 * STACK_DMAS * b + 16 * STACK_DMAS)
                for n in range(n0, n0 + count):
                    if not (first and n < 2):
                        pe.wait_ge(max_red, 16 * q + n - 1)
                    h, t = 4 * g + n // 4, n % 4
                    nc.tensor.matmul(p_max[:, n % 2, :], q_stack[0:MAX_ROW, h, t * P:(t + 1) * P],
                                     k_stack[0:MAX_ROW, h, :], start=True, stop=True).then_inc(max_mm, 1)

            def transpose_maxima(b, g):
                pe.wait_ge(max_red, 16 * (4 * b + g) + 16)
                nc.tensor.transpose(p_misc[0:16, 0:P], maxima[:, :], ident[:, :]).then_inc(max_t, 1)

            def scores(b, g, h, a, first):
                n = 8 * (4 * b + g) + 4 * a + h
                if h == 0 and a == 0:
                    pe.wait_ge(max_in, 32 * (4 * b + g) + 32)
                if not (first and g == 0 and a == 0 and h < 2):
                    pe.wait_ge(exp_done, n - 1)
                for j in range(2):
                    k = 2 * a + j
                    last = nc.tensor.matmul(p_score[:, 2 * (h % 2) + j, :], k_stack[0:STACK_ROWS, 4 * g + h, k * P:(k + 1) * P],
                                            q_stack[0:STACK_ROWS, 4 * g + h, :], start=True, stop=True)
                last.then_inc(score_mm, 1)

            def product_v(b, g, a, first):
                q = 4 * b + g
                pe.wait_ge(exp_done, 8 * q + 4 * a + 4)
                if a == 0:
                    pe.wait_ge(v_ready, 2 * b + g // 2 + 1)
                    if not first:
                        pe.wait_ge(av_out, q)
                for j in range(2):
                    for h in range(4):
                        last = nc.tensor.matmul(p_av[32 * h:32 * h + 32, :], v_rows[:, 2 * a + j, 4 * g + h, :],
                                                p_exp[:, a, h, j, :], start=(a == 0 and j == 0), stop=(a == 1 and j == 1))
                last.then_inc(av_done, 1)

            def transpose_y(q):
                pe.wait_ge(av_out, q + 1)
                for t in range(TT):
                    last = nc.tensor.transpose(p_misc[:, t * P:(t + 1) * P], av_sb[:, t * P:(t + 1) * P], ident[:, :])
                last.then_inc(y_t, 1)

            pe.wait_ge(consts_in, 96)
            pe.wait_ge(ident_in, 2)
            pe.wait_ge(setup, 8)
            for side, u in ((0, 0), (1, 0), (0, 1), (1, 1)):
                if side or u:
                    pe.wait_ge(qk_lo, 2 * u + side)
                project_qk(0, side, u)
            pe.wait_ge(qk_lo, 4)
            project_v(0, 0)
            max_tiles(0, 0, 0, 16, True)
            pe.wait_ge(v_ready, 1)
            transpose_maxima(0, 0)

            def body(b, first, last):
                misc = (max_lo_s, 4 * b + 1)
                for g in range(QUADS):
                    q = 4 * b + g
                    nb, ng = (b, g + 1) if g < 3 else (b + 1, 0)
                    n = 0
                    for step in plan(g, first, last):
                        if step[0] == "S":
                            scores(b, g, int(step[1]), "ab".index(step[2]), first)
                        elif step in ("M2", "M3"):
                            count = int(step[1])
                            max_tiles(nb, ng, n, count, False)
                            n += count
                        elif step == "AVb":
                            pb, pg = (b, g - 1) if g else (b - 1, 3)
                            product_v(pb, pg, 1, False)
                        elif step == "AVa":
                            product_v(b, g, 0, first and g == 0)
                        elif step == "Y":
                            pe.wait_ge(*misc)
                            transpose_y(q - 1)
                            misc = (y_norm, q)
                        elif step == "MT":
                            pe.wait_ge(*misc)
                            transpose_maxima(nb, ng)
                            misc = (max_lo_s, 4 * nb + ng + 1)
                        elif step == "V1":
                            pe.wait_ge(*misc)
                            project_v(b, 1)
                            misc = (v_ready, 2 * b + 2)
                        elif step == "V0":
                            pe.wait_ge(*misc)
                            project_v(b + 1, 0)
                            misc = (v_ready, 2 * b + 3)
                        else:
                            side, u = "QK".index(step[0]), int(step[1])
                            pe.wait_ge(*misc)
                            project_qk(b + 1, side, u)
                            misc = (qk_lo, 4 * (b + 1) + 2 * u + side + 1)

            batches(pe, body)
            product_v(B - 1, 3, 1, False)
            pe.wait_ge(y_norm, 4 * B - 1)
            transpose_y(4 * B - 1)

            pe.wait_ge(y_lo_s, 4 * B)

            def three_products(dst, w, cols, i, t):
                rows = bass.ds(t * 512, 512)
                for j in range(2):
                    for e in range(2):
                        k = 2 * j + e
                        c = slice(cols + j * P, cols + (j + 1) * P)
                        nc.tensor.matmul(dst, w[0][:, i, e, c], y_hi[:, k, rows], start=(k == 0), stop=False)
                        nc.tensor.matmul(dst, w[0][:, i, e, c], y_lo[:, k, rows], start=False, stop=False)
                        last = nc.tensor.matmul(dst, w[1][:, i, e, c], y_hi[:, k, rows], start=False, stop=(k == 3))
                return last

            def down(g, t, i, w):
                s = (g * CHUNKS + t) * UNITS + i
                pe.wait_ge(in_lo_s, s + 1)
                e, u = i % 2, i - i % 2
                w_hi, w_lo = (w[p][:, u:u + 2, e, 4 * P:4 * P + 256] for p in range(2))
                for r in range(4):
                    dst = p_out[:, r, :]
                    if i == 0 and not first_steps(s, 1):
                        pe.wait_ge(acc_add, 4 * (g * CHUNKS + t) - 3 + r)
                    rows = slice(r * P, (r + 1) * P)
                    nc.tensor.matmul(dst, in_hi[:, i % 2, rows], w_hi, start=(i == 0), stop=False)
                    nc.tensor.matmul(dst, in_hi[:, i % 2, rows], w_lo, start=False, stop=False)
                    last = nc.tensor.matmul(dst, in_lo[:, i % 2, rows], w_hi, start=False, stop=(i == UNITS - 1))
                    if i == UNITS - 1:
                        last.then_inc(sum_mm, 1)
                if i < UNITS - 1:
                    last.then_inc(down_mm, 1)

            def chunk(g, t):
                w = weights[g % 2]
                pe.wait_ge(w_lo_s, UNITS * (g + 1))
                for i in range(UNITS):
                    s = (g * CHUNKS + t) * UNITS + i
                    if not first_steps(s, 2):
                        pe.wait_ge(gelu_s, s - 1)
                    three_products(p_gate[i % 2], w, 0, i, t).then_inc(gate_mm, 1)
                    if not first_steps(s, 2):
                        pe.wait_ge(inter_s, s - 1)
                    three_products(p_up[i % 2], w, 2 * P, i, t).then_inc(up_mm, 1)
                    if i:
                        down(g, t, i - 1, w)
                down(g, t, UNITS - 1, w)

            chunks(pe, chunk)


def by_parity(a, axis):
    shape = a.shape
    a = a.reshape(*shape[:axis], shape[axis] // 256, 128, 2, *shape[axis + 1:])
    return a.swapaxes(axis + 1, axis + 2).reshape(shape)


def kernel(**inputs):
    import concourse.bacc as bacc
    import numpy as np
    from concourse.bass_utils import run_bass_kernel_spmd

    given = {k: np.asarray(v) for k, v in inputs.items()}

    def ffn_units(gate, up, down):
        r = gate.shape[0] // 2
        g, u = (a.reshape(2, r, F // P, P).transpose(2, 1, 0, 3).reshape(F // P, r, 2 * P) for a in (gate, up))
        d = down.reshape(F // 256, r, 2, 256).transpose(0, 2, 1, 3).reshape(F // P, r, 256)
        return np.ascontiguousarray(np.concatenate([g, u, d], axis=2))

    gate_w, up_w = (by_parity(given[f"L0_ffn_{n}_W_packed"], 0).T for n in ("gate", "up"))
    gate_s, up_s = (by_parity(given[f"L0_ffn_{n}_scales"], 0).T for n in ("gate", "up"))
    down_w, down_s = (by_parity(given[f"L0_ffn_down_{n}"], 0).T for n in ("W_packed", "scales"))
    arrays = {
        "x": by_parity(given["x"], 2),
        "mask": by_parity(given["cond_2048"], 1),
        "bias": given["L0_cond_b"],
        "wq": given["L0_cond_Wq"].T,
        "wk": given["L0_cond_Wk"].T,
        "wv": given["L0_cond_Wv"].T,
        "packed": ffn_units(gate_w, up_w, down_w).view(np.uint32),
        "scales": ffn_units(gate_s, up_s, down_s),
    }
    arrays = {k: np.ascontiguousarray(v) for k, v in arrays.items()}
    nc = bacc.Bacc("TRN2", target_bir_lowering=False, num_devices=1)
    args = {k: nc.dram_tensor(k, v.shape, mybir.dt.from_np(v.dtype), kind="ExternalInput").ap()
            for k, v in arrays.items()}
    out = nc.dram_tensor("out", (B * C, T), mybir.dt.float32, kind="ExternalOutput").ap()
    build(nc, out=out, **args)
    r = run_bass_kernel_spmd(nc, [arrays], core_ids=[0])
    got = r.results[0]["out"].reshape(B, C, T // 256, 2, 128)
    return np.ascontiguousarray(got.swapaxes(3, 4)).reshape(B, C, T)
```

```python
from contextlib import ExitStack

import concourse.bass as bass
import numpy as np
from concourse import mybir

P = 128
B, C, T = 8, 256, 512
F = 4096
NHEAD, DH = 16, 16
CK = C // P
TT = T // P
BLOCK = 32
QUADS = NHEAD // 4
UNIT_HEADS = P // DH

SEED_ROW = 64
MAX_ROW = 96
STACK_ROWS = 98
SEED_Q = 1024.0
MASK_K = 32768.0
MAX_K = 16.0
SCORE_SCALE = DH ** -0.5

Y_SCALE = 64.0
W_SCALE = 64.0
I_SCALE = 64.0
CODE_SCALE = 2.0 ** 14

GROUPS = 4
UNITS = F // P // GROUPS
CHUNKS = B * C // 512
WORDS = 2 * P + 2 * P + 256
DQ_STEPS = 4
STACK_DMAS = 5


def build(nc, x, mask, bias, wq, wk, wv, packed, scales, out):
    f32, f16, u32 = mybir.dt.float32, mybir.dt.float16, mybir.dt.uint32
    ALU, ACT, AX = mybir.AluOpType, mybir.ActivationFunctionType, mybir.AxisListType
    ctx = ExitStack()
    with ctx:
        def sb(name, shape, dt):
            return ctx.enter_context(nc.sbuf_tensor(name, shape, dt))

        def ps(name, shape, dt):
            return ctx.enter_context(nc.psum_tensor(name, shape, dt))

        def sem(name):
            return ctx.enter_context(nc.semaphore(name))

        y_hi = sb("y_hi", [P, TT, B * C], f16)
        y_lo = sb("y_lo", [P, TT, B * C], f16)
        w_even = [sb("w_even_hi", [P, UNITS, 2, WORDS], f16), sb("w_even_lo", [P, UNITS, 2, WORDS], f16)]
        dq_packed = sb("dq_packed", [P, WORDS], u32)
        dq_scales = sb("dq_scales", [P, WORDS], f32)
        dq_code = sb("dq_code", [P, WORDS], u32)
        dq_sign = sb("dq_sign", [P, WORDS], u32)
        dq_mag = sb("dq_mag", [P, WORDS], u32)
        dq_w = sb("dq_w", [P, 2, WORDS], f32)

        big = sb("big", [P, 8192], f32)
        p_exp = big[:, :].rearrange("p (a h k q) -> p a h k q", a=2, h=4, k=2)
        acc = big[:, :].rearrange("p (r h) -> p r h", h=T)
        wide = sb("wide", [P, 2 * UNITS * 2 * WORDS], f16)
        half = UNITS * 2 * WORDS
        w_odd = [wide[:, i * half:(i + 1) * half].rearrange("p (u e w) -> p u e w", u=UNITS, e=2) for i in range(2)]
        stack = NHEAD * T
        q_stack = wide[:, 0:stack].rearrange("p (h q) -> p h q", q=T)
        k_stack = wide[:, stack:2 * stack].rearrange("p (h q) -> p h q", q=T)
        v_words = TT * NHEAD * 32
        v_rows = wide[:, 2 * stack:2 * stack + 2 * v_words].bitcast(f32).rearrange(
            "p (k h d) -> p k h d", k=TT, h=NHEAD)
        parts = wide[:, 2 * stack + 2 * v_words:].rearrange("p (u n q) -> p u n q", u=2, q=T)
        qk = [[[parts[:, u, 2 * s + i, :] for i in range(2)] for u in range(2)] for s in range(2)]
        weights = [w_even, w_odd]

        small = sb("small", [P, 2560], f32)
        x_in = small[:, 0:1024].rearrange("p (k t) -> p k t", k=CK)
        w_proj = [small[:, 1024 + i * 512:1024 + (i + 1) * 512].rearrange("p (k o) -> p k o", k=CK) for i in range(3)]
        gelu = small[:, 0:1024].rearrange("p (i t) -> p i t", i=2)
        inter = small[:, 1024:2048].rearrange("p (i t) -> p i t", i=2)

        av_sb = sb("av_sb", [P, T], f32)
        y_f = sb("y_f", [P, TT, 64], f32)
        y_rec = sb("y_rec", [P, TT, 4], f32)
        maxima = sb("maxima", [P, 2, 16], f32)
        max_rows = [sb("max_hi", [16, P], f16), sb("max_lo", [16, P], f16)]
        ident = sb("ident", [P, P], f32)
        any_key = sb("any_key", [P, B], f32)
        any_now = sb("any_now", [P, 1], f32)
        in_hi = sb("in_hi", [P, 2, T], f16)
        in_lo = sb("in_lo", [P, 2, T], f16)

        mask_all = big[:, 0:B * T]
        mask_b = big[0:B, 4096:4608]
        mask_s = big[0:B, 4608:5120]
        any_b = big[0:B, 5120:5121]
        bias_b = big[0:B, 5121:5122]
        bias_s = big[0:B, 5122:5123]
        bias_hi = big[0:B, 5124:5125].bitcast(f16)[:, 0:1]
        bias_lo = big[0:B, 5125:5126]
        seed = big[0:B, 5632:5632 + 768].bitcast(f16).rearrange("b (r t) -> b r t", r=3)
        seed_dram = nc.dram_tensor("seed_rows", [B, 3, T], f16, kind="Internal").ap()

        qk_dram = nc.dram_tensor("qk_parts", [2, 4, DH, UNIT_HEADS, T], f16, kind="Internal").ap()

        psum = ps("psum", [P, 8, 512], f32)
        p_score, p_max, p_av, p_misc = psum[:, 0:4, :], psum[:, 4:6, :], psum[:, 6, :], psum[:, 7, :]
        p_gate, p_up, p_out = [psum[:, 0, :], psum[:, 2, :]], [psum[:, 1, :], psum[:, 3, :]], psum[:, 4:8, :]

        proj_in = [sem(f"proj_in{i}") for i in range(3)]
        ident_in = sem("ident_in")
        mask_in = sem("mask_in")
        masks_in = sem("masks_in")
        seed_in = sem("seed_in")
        setup = sem("setup")
        fixed = sem("fixed")
        dve_own = sem("dve_own")
        any_set = sem("any_set")
        seed_out = sem("seed_out")
        x_loaded = sem("x_loaded")
        qk_proj = sem("qk_proj")
        qk_hi = sem("qk_hi")
        qk_lo = sem("qk_lo")
        v_proj = sem("v_proj")
        v_ready = sem("v_ready")
        qk_out = [sem("qk_out0"), sem("qk_out1")]
        stack_in = [sem("stack_in0"), sem("stack_in1")]
        max_mm = sem("max_mm")
        max_red = sem("max_red")
        max_t = sem("max_t")
        max_hi_s = sem("max_hi_s")
        max_lo_s = sem("max_lo_s")
        max_in = sem("max_in")
        score_mm = sem("score_mm")
        exp_done = sem("exp_done")
        av_done = sem("av_done")
        av_out = sem("av_out")
        y_t = sem("y_t")
        y_rec_s = sem("y_rec_s")
        y_norm = sem("y_norm")
        y_hi_s = sem("y_hi_s")
        y_lo_s = sem("y_lo_s")
        dq_in = sem("dq_in")
        dq_step = sem("dq_step")
        scaled = sem("scaled")
        w_f_s = sem("w_f_s")
        w_hi_s = sem("w_hi_s")
        w_lo_s = sem("w_lo_s")
        acc_in = sem("acc_in")
        gate_mm = sem("gate_mm")
        up_mm = sem("up_mm")
        gelu_s = sem("gelu_s")
        inter_s = sem("inter_s")
        in_hi_s = sem("in_hi_s")
        in_lo_s = sem("in_lo_s")
        down_mm = sem("down_mm")
        sum_mm = sem("sum_mm")
        acc_add = sem("acc_add")
        stored = sem("stored")

        act_spare = nc.scalar.alloc_register("act_spare")
        pool_spare = nc.gpsimd.alloc_register("pool_spare")
        block = ctx.enter_context(nc.Block())

        AHEAD = 10
        PLAN = (
            "m S0a S1a m d0 F1 A2 m S2a m A3 m V1a ws m AO S3a m V1b V1h m S0b m S1b m Y MT X m MH ML S2b YN m S3b m Q0a A0 d1 m Q0b m A1 Q0h",
            "Q0l m S0a m K0a d2 m S1a m A2 m S2a m K0b m K0h S3a m A3 K0l AO m S0b m S1b MT m Y S2b YN MH m m ML S3b A0 F0 m m Q1a d3 Q1b m m A1 m Q1h",
            "S0a m A2 Q1l m S1a m A3 m AO m S2a K1a m S3a m Y m K1b YN K1h m S0b K1l S1b m A0 m MT MH S2b ML m S3b m A1",
            "m m wh A2 m A3 AO m m V0a S0a U m V0b m V0h S1a m m S2a m S3a m MT m S0b m Y MH YN ML m S1b m S2b A0 m S3b m A1 m",
        )
        WORK = ("Q0", "K0", "Q1", "K1", "V0", "V1")

        def plan(g, first, last):
            tile = AHEAD + sum(steps.split().count("m") for steps in PLAN[:g])
            for step in PLAN[g].split():
                if step in ("A2", "A3", "AO", "Y", "YN") and first and g == 0:
                    continue
                if step in ("MT", "MH", "ML") and last and g == QUADS - 1:
                    continue
                if last and (step in ("X", "F0") or step[0:2] in WORK and step[0:2] != "V1"):
                    continue
                if step == "m":
                    quad, at = 1 + tile // 16, tile % 16
                    tile += 1
                    if not (last and quad >= QUADS):
                        yield step, (quad, at)
                else:
                    yield step, None

        def of_batch(b, g):
            return (b, g) if g < 4 else (b + 1, g - 4)

        def batches(eng, body):
            body(0, True, False)
            with eng.Fori(1, B - 1) as b:
                body(b, False, False)
            body(B - 1, False, True)

        def wait_from(eng, sem, value):
            if not isinstance(value, int) or value > 0:
                eng.wait_ge(sem, value)

        def chunks(eng, body):
            for g in range(GROUPS):
                if g == 0:
                    body(0, 0)
                with eng.Fori(1 if g == 0 else 0, CHUNKS) as t:
                    body(g, t)

        def wait_apart(eng, spare, sem, value):
            eng.wait_ge(sem, value)
            eng.reg_mov(spare, 0)

        def unit_of(w, u):
            return w[:, u] if isinstance(u, int) else w[:, bass.ds(u, 1)].rearrange("p u e w -> p (u e) w")

        def pair(value):
            return float(np.array([value, value], np.float16).view(np.float32)[0])

        def load_x(sp, b):
            sp.dma_start(x_in, x[b].rearrange("(k p) t -> p k t", p=P)).then_inc(x_loaded, 16)

        def load_unit(sp, n, count):
            wait_from(sp, w_f_s, count)
            sp.dma_start(dq_packed[:, :], packed[n]).then_inc(dq_in, 16)
            sp.dma_start(dq_scales[:, :], scales[n].unsqueeze(1).broadcast_to([8, 16, WORDS])).then_inc(dq_in, 16)

        def store_qk(sp, b, u, side):
            sp.wait_ge(qk_lo, 4 * b + 2 * u + side + 1)
            for n in (2 * side, 2 * side + 1):
                sp.dma_start(qk_dram[u, n].rearrange("r h q -> h r q"), parts[:, u, n]).then_inc(qk_out[u], 16)

        def fill_stack(sp, b, u, first):
            sp.wait_ge(qk_out[u], 64 * b + 64)
            if not first:
                sp.wait_ge(score_mm, 32 * (b - 1) + 16 * u + 16)
            heads = slice(u * UNIT_HEADS, (u + 1) * UNIT_HEADS)
            for j in range(2):
                rows = slice(j * 2 * DH, (j + 1) * 2 * DH)
                sp.dma_start(q_stack[rows, heads, :],
                             qk_dram[u, j:j + 1].broadcast_to([2, DH, UNIT_HEADS, T])).then_inc(stack_in[u], 16)
                sp.dma_start(k_stack[rows, heads, :], qk_dram[u, 2:4]).then_inc(stack_in[u], 16)
            sp.dma_start(k_stack[SEED_ROW:SEED_ROW + 3, heads, :],
                         seed_dram[b].unsqueeze(1).broadcast_to([3, UNIT_HEADS, T])).then_inc(stack_in[u], 16)

        def move_max(sp, b, g):
            sp.wait_ge(max_lo_s, 4 * b + g + 1)
            for i in range(2):
                sp.dma_start(q_stack[MAX_ROW + i:MAX_ROW + i + 1, 4 * g:4 * g + 4, :].rearrange(
                    "o h (t q) -> o (h t) q", q=P), max_rows[i][:, :]).then_inc(max_in, 16)

        def weight_f(pool, n):
            pool.wait_ge(dq_step, DQ_STEPS * n + DQ_STEPS)
            pool.wait_ge(scaled, n + 1)
            wait_from(pool, w_lo_s, n)
            nc.gpsimd.tensor_tensor(dq_w[:, :, :], dq_code[:, :].bitcast(f16).rearrange("p (w e) -> p e w", e=2),
                                    dq_scales[:, :].unsqueeze(1).broadcast_to([P, 2, WORDS]),
                                    ALU.mult).then_inc(w_f_s, 1)

        def weight_scale(act, n):
            act.wait_ge(dq_in, 32 * n + 32)
            nc.scalar.activation(dq_scales[:, :], dq_scales[:, :], ACT.Copy,
                                 scale=CODE_SCALE * W_SCALE).then_inc(scaled, 1)

        def weight_lo(pool, n, w, u):
            wait_apart(pool, pool_spare, w_hi_s, n + 1)
            nc.gpsimd.tensor_tensor(unit_of(w[1], u), dq_w[:, :, :], unit_of(w[0], u),
                                    ALU.subtract).then_inc(w_lo_s, 1)

        def weight_hi(act, n, w, u):
            wait_apart(act, act_spare, w_f_s, n + 1)
            nc.scalar.copy(unit_of(w[0], u), dq_w[:, :, :]).then_inc(w_hi_s, 1)

        def decode(dve, n, k):
            done = DQ_STEPS * n
            if k == 0:
                dve.wait_ge(dq_in, 32 * n + 32)
                wait_from(dve, w_f_s, n)
                nc.vector.scalar_tensor_tensor(out=dq_code[:, :], in0=dq_packed[:, :], scalar=12, in1=dq_packed[:, :],
                                               op0=ALU.logical_shift_left, op1=ALU.bitwise_or).then_inc(dq_step, 1)
            elif k == 1:
                dve.wait_ge(dq_step, done + 1)
                nc.vector.tensor_scalar(dq_sign[:, :], dq_code[:, :], 12, 0x80008000, ALU.logical_shift_left,
                                        ALU.bitwise_and).then_inc(dq_step, 1)
            elif k == 2:
                nc.vector.tensor_scalar(dq_mag[:, :], dq_code[:, :], 9, 0x0E000E00, ALU.logical_shift_left,
                                        ALU.bitwise_and).then_inc(dq_step, 1)
            elif k == 3:
                dve.wait_ge(dq_step, done + 3)
                nc.vector.tensor_tensor(dq_code[:, :], dq_sign[:, :], dq_mag[:, :],
                                        ALU.bitwise_or).then_inc(dq_step, 1)

        @block.sync
        def _(sp):
            load_x(sp, 0)
            for i, w in enumerate((wq, wk, wv)):
                sp.dma_start(w_proj[i], w.rearrange("(k p) o -> p k o", p=P)).then_inc(proj_in[i], 16)
            load_unit(sp, 0, 0)
            sp.wait_ge(setup, 3)
            sp.wait_ge(fixed, 2)
            sp.dma_start(seed_dram, seed).then_inc(seed_out, 16)
            sp.wait_ge(seed_out, 16)
            store_qk(sp, 0, 0, 0)
            store_qk(sp, 0, 0, 1)
            fill_stack(sp, 0, 0, True)
            move_max(sp, 0, 0)

            def body(b, first, last):
                for g in range(QUADS):
                    for step, _ in plan(g, first, last):
                        if step == "ML":
                            move_max(sp, *of_batch(b, g + 1))
                        elif step == "X":
                            sp.wait_ge(v_proj, 2 * b + 2)
                            load_x(sp, b + 1)
                        elif step[0:2] in WORK and step[0] != "V" and step[2] == "l":
                            store_qk(sp, b + 1, int(step[1]), "QK".index(step[0]))
                        elif step == "F0":
                            fill_stack(sp, b + 1, 0, False)
                        elif step == "F1":
                            fill_stack(sp, b, 1, first)
                        elif step == "U":
                            load_unit(sp, b + 1, b + 1)

            batches(sp, body)

            sp.wait_ge(av_done, 8 * B)
            for r in range(CHUNKS):
                sp.dma_start(acc[:, 4 * r:4 * r + 4, :],
                             x.rearrange("b (k p) t -> p (b k) t", p=P)[:, 4 * r:4 * r + 4, :]).then_inc(acc_in, 16)
            with sp.Fori(UNITS + 1, GROUPS * UNITS) as n:
                load_unit(sp, n, n)
            for r in range(4 * CHUNKS):
                sp.wait_ge(acc_add, 4 * (GROUPS - 1) * CHUNKS + r + 1)
                sp.dma_start(out[r * P:(r + 1) * P, :], acc[:, r, :]).then_inc(stored, 16)
            sp.wait_ge(stored, 16 * 4 * CHUNKS)

        @block.gpsimd
        def _(pool):
            nc.gpsimd.memset(k_stack[SEED_ROW:MAX_ROW, :, :].bitcast(f32), 0.0).then_inc(fixed, 1)
            pool.wait_ge(fixed, 1)
            nc.gpsimd.memset(k_stack[MAX_ROW:STACK_ROWS, :, :].bitcast(f32), pair(MAX_K)).then_inc(fixed, 1)
            pool.wait_ge(fixed, 2)
            nc.gpsimd.memset(v_rows[:, :, :, :], 0.0).then_inc(fixed, 1)
            pool.wait_ge(fixed, 3)
            nc.gpsimd.memset(v_rows[:, :, :, DH:DH + 1], 1.0 / Y_SCALE).then_inc(fixed, 1)
            pool.wait_ge(fixed, 4)
            nc.gpsimd.memset(ident[:, :], 0.0).then_inc(ident_in, 1)
            pool.wait_ge(ident_in, 1)
            nc.gpsimd.affine_select(out=ident[:, :], in_=ident[:, :], compare_op=ALU.not_equal, fill=1.0, base=0,
                                    pattern=[[-1, P]], channel_multiplier=1).then_inc(ident_in, 1)

            def split_y(b, g):
                q = 4 * b + g
                cols = bass.ds(b * C + g * 64, 64)
                wait_apart(pool, pool_spare, y_norm, q + 1)
                nc.gpsimd.tensor_copy(y_hi[:, :, cols], y_f[:, :, :]).then_inc(y_hi_s, 1)
                wait_apart(pool, pool_spare, y_hi_s, q + 1)
                nc.gpsimd.tensor_tensor(y_lo[:, :, cols], y_f[:, :, :], y_hi[:, :, cols],
                                        ALU.subtract).then_inc(y_lo_s, 1)

            def body(b, first, last):
                if not first:
                    split_y(b - 1, 3)
                for g in range(3):
                    split_y(b, g)
                    if g == 0:
                        weight_f(pool, b)
                    if g == 2:
                        weight_lo(pool, b, weights[0], b)

            batches(pool, body)
            split_y(B - 1, 3)

            for g in range(GROUPS - 1):
                with pool.Fori(0, CHUNKS) as t:
                    for i in range(2):
                        weight_f(pool, (g + 1) * UNITS + 2 * t + i)
                        weight_lo(pool, (g + 1) * UNITS + 2 * t + i, weights[(g + 1) % 2], 2 * t + i)

        @block.scalar
        def _(act):
            def qk_part(b, side, u, first, bank):
                n = 4 * b + 2 * u + side
                if not first:
                    act.wait_ge(qk_out[u], 64 * b)
                    if side == 0 and u == 0:
                        act.wait_ge(any_set, b + 1)
                act.wait_ge(qk_proj, n + 1)
                scale = 1.0 if side else any_now[:, :]
                nc.scalar.activation(qk[side][u][0], bank, ACT.Copy, scale=scale).then_inc(qk_hi, 1)

            def v_part(b, u, first):
                act.wait_ge(v_proj, 2 * b + u + 1)
                if not first:
                    act.wait_ge(av_done, 8 * (b - 1) + 4 * u + 4)
                nc.scalar.activation(v_rows[:, :, u * UNIT_HEADS:(u + 1) * UNIT_HEADS, 0:DH],
                                     p_misc.rearrange("p (k h d) -> p k h d", k=TT, h=UNIT_HEADS),
                                     ACT.Copy).then_inc(v_ready, 1)

            def max_part(b, g, first):
                q = 4 * b + g
                act.wait_ge(max_t, q + 1)
                if not (first and g == 0):
                    act.wait_ge(max_in, 32 * q)
                nc.scalar.activation(max_rows[0][:, :], p_misc[0:16, 0:P], ACT.Copy,
                                     scale=-1.0 / MAX_K).then_inc(max_hi_s, 1)

            act.dma_start(mask_all[:, 0:T], mask[0].partition_broadcast(P)).then_inc(mask_in, 16)
            act.dma_start(mask_b, mask).then_inc(seed_in, 16)
            act.dma_start(bias_b, bias.partition_broadcast(B)).then_inc(seed_in, 16)
            act.dma_start(mask_all[:, T:], mask[1:].rearrange("b t -> (b t)").partition_broadcast(P)).then_inc(masks_in, 16)
            act.wait_ge(any_set, 1)
            for u in range(2):
                for side in range(2):
                    qk_part(0, side, u, True, psum[:, 2 * u + side, :])
            act.wait_ge(fixed, 4)
            v_part(0, 0, True)
            store_qk(act, 0, 1, 0)
            store_qk(act, 0, 1, 1)
            max_part(0, 0, True)

            def body(b, first, last):
                for g in range(QUADS):
                    q = 4 * b + g
                    for step, arg in plan(g, first, last):
                        if step[0] == "S":
                            h, a = int(step[1]), "ab".index(step[2])
                            act.wait_ge(score_mm, 8 * q + 4 * a + h + 1)
                            wait_from(act, av_done, 2 * q - 1 + a)
                            nc.scalar.activation(p_exp[:, a, h], p_score[:, 2 * (h % 2):2 * (h % 2) + 2, :], ACT.Exp,
                                                 scale=SCORE_SCALE).then_inc(exp_done, 1)
                        elif step == "AO":
                            copy_av(q - 1)
                        elif step == "MH":
                            max_part(*of_batch(b, g + 1), False)
                        elif step[0:2] in WORK and step[2] == "h":
                            u = int(step[1])
                            if step[0] == "V":
                                v_part(b + 1 - u, u, first and u == 1)
                            else:
                                qk_part(b + 1, "QK".index(step[0]), u, False, p_misc)
                        elif step == "ws":
                            weight_scale(act, b)
                        elif step == "wh":
                            weight_hi(act, b, weights[0], b)

            def copy_av(q):
                act.wait_ge(av_done, 2 * q + 2)
                wait_from(act, y_t, q)
                nc.scalar.copy(av_sb[:, :], p_av).then_inc(av_out, 1)

            batches(act, body)
            copy_av(4 * B - 1)

            def chunk(g, t):
                for i in range(UNITS):
                    s = (g * CHUNKS + t) * UNITS + i
                    act.wait_ge(gate_mm, s + 1)
                    wait_from(act, inter_s, s - 1)
                    nc.scalar.activation(gelu[:, i % 2, :], p_gate[i % 2], ACT.Gelu_apprx_tanh,
                                         scale=1.0 / (Y_SCALE * W_SCALE)).then_inc(gelu_s, 1)
                    act.wait_ge(inter_s, s + 1)
                    c = g * CHUNKS + t
                    if i >= 2:
                        act.wait_ge(down_mm, (UNITS - 1) * c + i - 1)
                    elif i == 0:
                        wait_from(act, down_mm, (UNITS - 1) * c)
                    else:
                        wait_from(act, sum_mm, 4 * c)
                    nc.scalar.copy(in_hi[:, i % 2, :], inter[:, i % 2, :]).then_inc(in_hi_s, 1)
                    if g < GROUPS - 1 and i % 4 == 0:
                        weight_scale(act, (g + 1) * UNITS + 2 * t + i // 4)
                    if g < GROUPS - 1 and i % 4 == 3:
                        u = 2 * t + i // 4
                        weight_hi(act, (g + 1) * UNITS + u, weights[(g + 1) % 2], u)

            chunks(act, chunk)

        @block.vector
        def _(dve):
            nc.vector.memset(q_stack[SEED_ROW:MAX_ROW, :, :].bitcast(f32), pair(SEED_Q)).then_inc(setup, 1)
            dve.wait_ge(mask_in, 16)
            nc.vector.reduce_max(any_now[:, :], mask_all[:, 0:T], AX.X).then_inc(any_set, 1)
            dve.wait_ge(seed_in, 32)
            nc.vector.reduce_max(any_b, mask_b, AX.X).then_inc(dve_own, 1)
            nc.vector.tensor_scalar(mask_s, mask_b, 1.0, MASK_K, ALU.subtract, ALU.mult).then_inc(dve_own, 1)
            nc.vector.tensor_scalar(bias_s, bias_b, 1.0 / (SCORE_SCALE * SEED_Q), None, ALU.mult).then_inc(dve_own, 1)
            dve.wait_ge(dve_own, 3)
            nc.vector.tensor_scalar(seed[:, 0, :], mask_s, any_b, None, ALU.mult).then_inc(dve_own, 1)
            nc.vector.tensor_scalar(bias_s, bias_s, any_b, None, ALU.mult).then_inc(dve_own, 1)
            dve.wait_ge(dve_own, 5)
            nc.vector.tensor_copy(bias_hi, bias_s).then_inc(dve_own, 1)
            dve.wait_ge(dve_own, 6)
            nc.vector.tensor_tensor(bias_lo, bias_s, bias_hi, ALU.subtract).then_inc(dve_own, 1)
            nc.vector.tensor_scalar(mask_s, mask_b, 0.0, None, ALU.mult).then_inc(dve_own, 1)
            dve.wait_ge(dve_own, 8)
            nc.vector.tensor_scalar(seed[:, 1, :], mask_s, bias_hi, None, ALU.add).then_inc(setup, 1)
            nc.vector.tensor_scalar(seed[:, 2, :], mask_s, bias_lo, None, ALU.add).then_inc(setup, 1)

            def qk_part(b, side, u, bank):
                n = 4 * b + 2 * u + side
                dve.wait_ge(qk_hi, n + 1)
                scale = 1.0 if side else any_now[:, :]
                nc.vector.scalar_tensor_tensor(out=qk[side][u][1], in0=bank, scalar=scale, in1=qk[side][u][0],
                                               op0=ALU.mult, op1=ALU.subtract).then_inc(qk_lo, 1)

            def reduce_maximum(b, g, n):
                q = 4 * b + g
                if n == 0:
                    wait_from(dve, max_t, q - 1)
                dve.wait_ge(max_mm, 16 * q + n + 1)
                nc.vector.reduce_max(maxima[:, g % 2, n:n + 1], p_max[:, n % 2, :], AX.X).then_inc(max_red, 1)

            def max_part(b, g):
                q = 4 * b + g
                dve.wait_ge(max_hi_s, q + 1)
                nc.vector.scalar_tensor_tensor(out=max_rows[1][:, :], in0=p_misc[0:16, 0:P], scalar=-1.0 / MAX_K,
                                               in1=max_rows[0][:, :], op0=ALU.mult,
                                               op1=ALU.subtract).then_inc(max_lo_s, 1)

            def normalise(q):
                dve.wait_ge(y_t, q + 1)
                nc.vector.reciprocal(y_rec[:, :, :], y_rows[:, :, :, DH]).then_inc(y_rec_s, 1)
                dve.wait_ge(y_rec_s, q + 1)
                wait_from(dve, y_lo_s, q)
                nc.vector.tensor_tensor(y_f[:, :, :].rearrange("p k (h d) -> p k h d", h=4), y_rows[:, :, :, 0:DH],
                                        y_rec[:, :, :].unsqueeze(3).broadcast_to([P, TT, 4, DH]),
                                        ALU.mult).then_inc(y_norm, 1)

            y_rows = p_av.rearrange("p (k h d) -> p k h d", k=TT, h=4)
            for side, u in ((0, 0), (1, 0), (0, 1), (1, 1)):
                qk_part(0, side, u, psum[:, 2 * u + side, :])
            dve.wait_ge(masks_in, 16)
            nc.vector.reduce_max(any_key[:, :], mask_all.rearrange("p (b t) -> p b t", b=B), AX.X).then_inc(dve_own, 1)
            dve.wait_ge(dve_own, 9)
            for n in range(16):
                reduce_maximum(0, 0, n)
            max_part(0, 0)
            for n in range(AHEAD):
                reduce_maximum(0, 1, n)

            def body(b, first, last):
                if not last:
                    nc.vector.tensor_copy(any_now[:, :], any_key[:, bass.ds(b + 1, 1)]).then_inc(any_set, 1)
                for g in range(QUADS):
                    for step, arg in plan(g, first, last):
                        if step == "m":
                            reduce_maximum(*of_batch(b, arg[0]), arg[1])
                        elif step == "ML":
                            max_part(*of_batch(b, g + 1))
                        elif step == "YN":
                            normalise(4 * b + g - 1)
                        elif step[0:2] in WORK and step[2] == "l":
                            qk_part(b + 1, "QK".index(step[0]), int(step[1]), p_misc)
                        elif step[0] == "d":
                            decode(dve, b, int(step[1]))

            batches(dve, body)
            normalise(4 * B - 1)

            def chunk(g, t):
                for i in range(UNITS):
                    s = (g * CHUNKS + t) * UNITS + i
                    dve.wait_ge(gelu_s, s + 1)
                    dve.wait_ge(up_mm, s + 1)
                    wait_from(dve, in_lo_s, s - 1)
                    nc.vector.scalar_tensor_tensor(out=inter[:, i % 2, :], in0=p_up[i % 2],
                                                   scalar=I_SCALE / (Y_SCALE * W_SCALE), in1=gelu[:, i % 2, :],
                                                   op0=ALU.mult, op1=ALU.mult).then_inc(inter_s, 1)
                    dve.wait_ge(in_hi_s, s + 1)
                    nc.vector.tensor_tensor(in_lo[:, i % 2, :], inter[:, i % 2, :], in_hi[:, i % 2, :],
                                            ALU.subtract).then_inc(in_lo_s, 1)
                    if g < GROUPS - 1:
                        for k in ((0,), (1, 2), (3,), ())[i % 4]:
                            decode(dve, (g + 1) * UNITS + 2 * t + i // 4, k)
                c = g * CHUNKS + t
                for r in range(4):
                    dve.wait_ge(sum_mm, 4 * c + r + 1)
                    if g == 0:
                        dve.wait_ge(acc_in, 16 * CHUNKS)
                    rows = acc[:, bass.ds(4 * t + r, 1), :].rearrange("p r h -> p (r h)")
                    if g > 0:
                        dve.wait_ge(acc_add, 4 * (c - CHUNKS) + r + 1)
                    nc.vector.scalar_tensor_tensor(out=rows, in0=p_out[:, r, :], scalar=1.0 / (I_SCALE * W_SCALE),
                                                   in1=rows, op0=ALU.mult, op1=ALU.add).then_inc(acc_add, 1)

            chunks(dve, chunk)

        @block.tensor
        def _(pe):
            def project_qk(b, side, u, k, bank):
                if side == 0 and u == 0 and k == 0:
                    pe.wait_ge(x_loaded, 16 * b + 16)
                last = nc.tensor.matmul(bank, w_proj[side][:, k, u * P:(u + 1) * P], x_in[:, k, :],
                                        start=(k == 0), stop=(k == CK - 1))
                if k == CK - 1:
                    last.then_inc(qk_proj, 1)

            def project_v(b, u, i):
                for t in (2 * i, 2 * i + 1):
                    for k in range(CK):
                        last = nc.tensor.matmul(p_misc[:, t * P:(t + 1) * P], x_in[:, k, t * P:(t + 1) * P],
                                                w_proj[2][:, k, u * P:(u + 1) * P], start=(k == 0), stop=(k == CK - 1))
                if i == 1:
                    last.then_inc(v_proj, 1)

            def max_tile(b, g, n):
                if n == 0:
                    pe.wait_ge(stack_in[g // 2], 16 * STACK_DMAS * b + 16 * STACK_DMAS)
                wait_from(pe, max_red, 16 * (4 * b + g) + n - 1)
                h, t = 4 * g + n // 4, n % 4
                nc.tensor.matmul(p_max[:, n % 2, :], q_stack[0:MAX_ROW, h, t * P:(t + 1) * P],
                                 k_stack[0:MAX_ROW, h, :], start=True, stop=True).then_inc(max_mm, 1)

            def transpose_maxima(b, g):
                pe.wait_ge(max_red, 16 * (4 * b + g) + 16)
                nc.tensor.transpose(p_misc[0:16, 0:P], maxima[:, g % 2, :], ident[:, :]).then_inc(max_t, 1)

            def scores(b, g, h, a):
                n = 8 * (4 * b + g) + 4 * a + h
                if h == 0 and a == 0:
                    pe.wait_ge(max_in, 32 * (4 * b + g) + 32)
                wait_from(pe, exp_done, n - 1)
                for j in range(2):
                    k = 2 * a + j
                    last = nc.tensor.matmul(p_score[:, 2 * (h % 2) + j, :], k_stack[0:STACK_ROWS, 4 * g + h, k * P:(k + 1) * P],
                                            q_stack[0:STACK_ROWS, 4 * g + h, :], start=True, stop=True)
                last.then_inc(score_mm, 1)

            def product_v(b, g, k):
                q, a, j = 4 * b + g, k // 2, k % 2
                if j == 0:
                    pe.wait_ge(exp_done, 8 * q + 4 * a + 4)
                if k == 0:
                    pe.wait_ge(v_ready, 2 * b + g // 2 + 1)
                    wait_from(pe, y_norm, q)
                for h in range(4):
                    last = nc.tensor.matmul(p_av[32 * h:32 * h + 32, :], v_rows[:, k, 4 * g + h, :],
                                            p_exp[:, a, h, j, :], start=(k == 0), stop=(k == TT - 1))
                if j == 1:
                    last.then_inc(av_done, 1)

            def transpose_y(q):
                pe.wait_ge(av_out, q + 1)
                for t in range(TT):
                    last = nc.tensor.transpose(p_av[:, t * P:(t + 1) * P], av_sb[:, t * P:(t + 1) * P], ident[:, :])
                last.then_inc(y_t, 1)

            for u in range(2):
                for side in range(2):
                    pe.wait_ge(proj_in[side], 16)
                    for k in range(CK):
                        project_qk(0, side, u, k, psum[:, 2 * u + side, :])
            pe.wait_ge(proj_in[2], 16)
            for i in range(2):
                project_v(0, 0, i)
            for n in range(16):
                max_tile(0, 0, n)
            pe.wait_ge(v_ready, 1)
            pe.wait_ge(ident_in, 2)
            transpose_maxima(0, 0)
            for n in range(AHEAD):
                max_tile(0, 1, n)

            def body(b, first, last):
                misc = (max_lo_s, 4 * b + 1)
                for g in range(QUADS):
                    q = 4 * b + g
                    for step, arg in plan(g, first, last):
                        if step[0] == "S":
                            scores(b, g, int(step[1]), "ab".index(step[2]))
                        elif step == "m":
                            max_tile(*of_batch(b, arg[0]), arg[1])
                        elif step in ("A2", "A3"):
                            product_v(*((b, g - 1) if g else (b - 1, 3)), int(step[1]))
                        elif step in ("A0", "A1"):
                            product_v(b, g, int(step[1]))
                        elif step == "Y":
                            transpose_y(q - 1)
                        elif step == "MT":
                            pe.wait_ge(*misc)
                            transpose_maxima(*of_batch(b, g + 1))
                            misc = (max_lo_s, q + 2)
                        elif step[0:2] in WORK and step[2] in "ab":
                            u, piece = int(step[1]), "ab".index(step[2])
                            if piece == 0:
                                pe.wait_ge(*misc)
                            if step[0] == "V":
                                project_v(b + 1 - u, u, piece)
                                misc = (v_ready, 2 * (b + 1 - u) + u + 1)
                            else:
                                side = "QK".index(step[0])
                                project_qk(b + 1, side, u, piece, p_misc)
                                misc = (qk_lo, 4 * (b + 1) + 2 * u + side + 1)

            batches(pe, body)
            product_v(B - 1, 3, 2)
            product_v(B - 1, 3, 3)

            def three_products(dst, w, cols, i, t):
                rows = bass.ds(t * 512, 512)
                for j in range(2):
                    for e in range(2):
                        k = 2 * j + e
                        c = slice(cols + j * P, cols + (j + 1) * P)
                        nc.tensor.matmul(dst, w[0][:, i, e, c], y_hi[:, k, rows], start=(k == 0), stop=False)
                        nc.tensor.matmul(dst, w[0][:, i, e, c], y_lo[:, k, rows], start=False, stop=False)
                        last = nc.tensor.matmul(dst, w[1][:, i, e, c], y_hi[:, k, rows], start=False, stop=(k == 3))
                return last

            def down(g, t, i, w):
                s = (g * CHUNKS + t) * UNITS + i
                pe.wait_ge(in_lo_s, s + 1)
                e, u = i % 2, i - i % 2
                w_hi, w_lo = (w[p][:, u:u + 2, e, 4 * P:4 * P + 256] for p in range(2))
                for r in range(4):
                    dst = p_out[:, r, :]
                    if i == 0:
                        wait_from(pe, acc_add, 4 * (g * CHUNKS + t) - 3 + r)
                    rows = slice(r * P, (r + 1) * P)
                    nc.tensor.matmul(dst, in_hi[:, i % 2, rows], w_hi, start=(i == 0), stop=False)
                    nc.tensor.matmul(dst, in_hi[:, i % 2, rows], w_lo, start=False, stop=False)
                    last = nc.tensor.matmul(dst, in_lo[:, i % 2, rows], w_hi, start=False, stop=(i == UNITS - 1))
                    if i == UNITS - 1:
                        last.then_inc(sum_mm, 1)
                if i < UNITS - 1:
                    last.then_inc(down_mm, 1)

            def chunk(g, t):
                w = weights[g % 2]
                start = isinstance(t, int) and g == t == 0
                if g == 0:
                    pe.wait_ge(y_lo_s, 8 * t + 8)
                if start:
                    pe.wait_ge(exp_done, 32 * B)
                if not start:
                    pe.wait_ge(w_lo_s, UNITS * (g + 1))
                for i in range(UNITS):
                    s = (g * CHUNKS + t) * UNITS + i
                    if start:
                        pe.wait_ge(w_lo_s, i + 1)
                    if start and i == 1:
                        transpose_y(4 * B - 1)
                        pe.wait_ge(y_norm, 4 * B)
                    wait_from(pe, gelu_s, s - 1)
                    three_products(p_gate[i % 2], w, 0, i, t).then_inc(gate_mm, 1)
                    wait_from(pe, inter_s, s - 1)
                    three_products(p_up[i % 2], w, 2 * P, i, t).then_inc(up_mm, 1)
                    if i:
                        down(g, t, i - 1, w)
                down(g, t, UNITS - 1, w)

            chunks(pe, chunk)


def by_parity(a, axis):
    shape = a.shape
    a = a.reshape(*shape[:axis], shape[axis] // 256, 128, 2, *shape[axis + 1:])
    return a.swapaxes(axis + 1, axis + 2).reshape(shape)


def kernel(**inputs):
    import concourse.bacc as bacc
    import numpy as np
    from concourse.bass_utils import run_bass_kernel_spmd

    given = {k: np.asarray(v) for k, v in inputs.items()}

    def ffn_units(gate, up, down):
        r = gate.shape[0] // 2
        g, u = (a.reshape(2, r, F // P, P).transpose(2, 1, 0, 3).reshape(F // P, r, 2 * P) for a in (gate, up))
        d = down.reshape(F // 256, r, 2, 256).transpose(0, 2, 1, 3).reshape(F // P, r, 256)
        return np.ascontiguousarray(np.concatenate([g, u, d], axis=2))

    gate_w, up_w = (by_parity(given[f"L0_ffn_{n}_W_packed"], 0).T for n in ("gate", "up"))
    gate_s, up_s = (by_parity(given[f"L0_ffn_{n}_scales"], 0).T for n in ("gate", "up"))
    down_w, down_s = (by_parity(given[f"L0_ffn_down_{n}"], 0).T for n in ("W_packed", "scales"))
    arrays = {
        "x": by_parity(given["x"], 2),
        "mask": by_parity(given["cond_2048"], 1),
        "bias": given["L0_cond_b"],
        "wq": given["L0_cond_Wq"].T,
        "wk": given["L0_cond_Wk"].T,
        "wv": given["L0_cond_Wv"].T,
        "packed": ffn_units(gate_w, up_w, down_w).view(np.uint32),
        "scales": ffn_units(gate_s, up_s, down_s),
    }
    arrays = {k: np.ascontiguousarray(v) for k, v in arrays.items()}
    nc = bacc.Bacc("TRN2", target_bir_lowering=False, num_devices=1)
    args = {k: nc.dram_tensor(k, v.shape, mybir.dt.from_np(v.dtype), kind="ExternalInput").ap()
            for k, v in arrays.items()}
    out = nc.dram_tensor("out", (B * C, T), mybir.dt.float32, kind="ExternalOutput").ap()
    build(nc, out=out, **args)
    r = run_bass_kernel_spmd(nc, [arrays], core_ids=[0])
    got = r.results[0]["out"].reshape(B, C, T // 256, 2, 128)
    return np.ascontiguousarray(got.swapaxes(3, 4)).reshape(B, C, T)
```

```python
from contextlib import ExitStack

import concourse.bass as bass
import numpy as np
from concourse import mybir

P = 128
B, C, T = 8, 256, 512
F = 4096
NHEAD, DH = 16, 16
CK = C // P
TT = T // P
BLOCK = 32
QUADS = NHEAD // 4
UNIT_HEADS = P // DH

SEED_ROW = 64
MAX_ROW = 96
STACK_ROWS = 98
SEED_Q = 1024.0
MASK_K = 32768.0
MAX_K = 16.0
SCORE_SCALE = DH ** -0.5

Y_SCALE = 64.0
W_SCALE = 64.0
I_SCALE = 64.0
CODE_SCALE = 2.0 ** 14

GROUPS = 4
UNITS = F // P // GROUPS
CHUNKS = B * C // 512
WORDS = 2 * P + 2 * P + 256
DQ_STEPS = 4
STACK_DMAS = 5


def build(nc, x, mask, bias, wq, wk, wv, packed, scales, out):
    f32, f16, u32 = mybir.dt.float32, mybir.dt.float16, mybir.dt.uint32
    ALU, ACT, AX = mybir.AluOpType, mybir.ActivationFunctionType, mybir.AxisListType
    ctx = ExitStack()
    with ctx:
        def sb(name, shape, dt):
            return ctx.enter_context(nc.sbuf_tensor(name, shape, dt))

        def ps(name, shape, dt):
            return ctx.enter_context(nc.psum_tensor(name, shape, dt))

        def sem(name):
            return ctx.enter_context(nc.semaphore(name))

        y_hi = sb("y_hi", [P, TT, B * C], f16)
        y_lo = sb("y_lo", [P, TT, B * C], f16)
        w_even = [sb("w_even_hi", [P, UNITS, 2, WORDS], f16), sb("w_even_lo", [P, UNITS, 2, WORDS], f16)]
        dq_packed = sb("dq_packed", [P, WORDS], u32)
        dq_scales = sb("dq_scales", [P, WORDS], f32)
        dq_code = sb("dq_code", [P, WORDS], u32)
        dq_sign = sb("dq_sign", [P, WORDS], u32)
        dq_mag = sb("dq_mag", [P, WORDS], u32)
        dq_w = sb("dq_w", [P, 2, WORDS], f32)

        big = sb("big", [P, 8192], f32)
        p_exp = big[:, :].rearrange("p (a h k q) -> p a h k q", a=2, h=4, k=2)
        acc = big[:, :].rearrange("p (r h) -> p r h", h=T)
        wide = sb("wide", [P, 2 * UNITS * 2 * WORDS], f16)
        half = UNITS * 2 * WORDS
        w_odd = [wide[:, i * half:(i + 1) * half].rearrange("p (u e w) -> p u e w", u=UNITS, e=2) for i in range(2)]
        stack = NHEAD * T
        q_stack = wide[:, 0:stack].rearrange("p (h q) -> p h q", q=T)
        k_stack = wide[:, stack:2 * stack].rearrange("p (h q) -> p h q", q=T)
        v_words = TT * NHEAD * 32
        v_rows = wide[:, 2 * stack:2 * stack + 2 * v_words].bitcast(f32).rearrange(
            "p (k h d) -> p k h d", k=TT, h=NHEAD)
        parts = wide[:, 2 * stack + 2 * v_words:].rearrange("p (u n q) -> p u n q", u=2, q=T)
        qk = [[[parts[:, u, 2 * s + i, :] for i in range(2)] for u in range(2)] for s in range(2)]  
        weights = [w_even, w_odd]

        small = sb("small", [P, 2560], f32)
        x_in = small[:, 0:1024].rearrange("p (k t) -> p k t", k=CK)
        w_parts = [[small[:, 1024 + i * 512:1024 + (i + 1) * 512].bitcast(f16).rearrange(
            "p (e k o) -> p e k o", e=2, k=CK)[:, e] for e in range(2)] for i in range(3)]
        gelu = small[:, 0:1024].rearrange("p (i t) -> p i t", i=2)
        inter = small[:, 1024:2048].rearrange("p (i t) -> p i t", i=2)

        av_sb = sb("av_sb", [P, T], f32)
        y_f = sb("y_f", [P, TT, 64], f32)
        y_rec = sb("y_rec", [P, TT, 4], f32)
        maxima = sb("maxima", [P, 2, 16], f32)
        max_rows = [sb("max_hi", [16, P], f16), sb("max_lo", [16, P], f16)]
        ident = sb("ident", [P, P], f32)
        any_key = sb("any_key", [P, B], f32)
        any_now = sb("any_now", [P, 1], f32)
        in_hi = sb("in_hi", [P, 2, T], f16)
        in_lo = sb("in_lo", [P, 2, T], f16)
        x_parts = [in_hi, in_lo]

        w_proj = [big[:, 6400 + i * 512:6400 + (i + 1) * 512].rearrange("p (k o) -> p k o", k=CK) for i in range(3)]
        mask_all = big[:, 0:B * T]
        mask_b = big[0:B, 4096:4608]
        mask_s = big[0:B, 4608:5120]
        any_b = big[0:B, 5120:5121]
        bias_b = big[0:B, 5121:5122]
        bias_s = big[0:B, 5122:5123]
        bias_hi = big[0:B, 5124:5125].bitcast(f16)[:, 0:1]
        bias_lo = big[0:B, 5125:5126]
        seed = big[0:B, 5632:5632 + 768].bitcast(f16).rearrange("b (r t) -> b r t", r=3)
        seed_dram = nc.dram_tensor("seed_rows", [B, 3, T], f16, kind="Internal").ap()

        qk_dram = nc.dram_tensor("qk_parts", [2, 4, DH, UNIT_HEADS, T], f16, kind="Internal").ap()

        psum = ps("psum", [P, 8, 512], f32)
        p_score, p_max, p_av, p_misc = psum[:, 0:4, :], psum[:, 4:6, :], psum[:, 6, :], psum[:, 7, :]
        p_gate, p_up = [psum[:, 4, :], psum[:, 0, :]], [psum[:, 5, :], psum[:, 1, :]]
        p_out = [psum[:, n, :] for n in (2, 3, 6, 7)]

        proj_in = [sem(f"proj_in{i}") for i in range(3)]
        ident_in = sem("ident_in")
        mask_in = sem("mask_in")
        masks_in = sem("masks_in")
        seed_in = sem("seed_in")
        setup = sem("setup")
        fixed = sem("fixed")
        dve_own = sem("dve_own")
        any_set = sem("any_set")
        seed_out = sem("seed_out")
        x_loaded = sem("x_loaded")
        x_hi_s = sem("x_hi_s")
        x_lo_s = sem("x_lo_s")
        wp_hi_s = sem("wp_hi_s")
        wp_lo_s = sem("wp_lo_s")
        qk_proj = sem("qk_proj")
        qk_hi = sem("qk_hi")
        qk_lo = sem("qk_lo")
        v_proj = sem("v_proj")
        v_ready = sem("v_ready")
        qk_out = [sem("qk_out0"), sem("qk_out1")]
        stack_in = [sem("stack_in0"), sem("stack_in1")]
        max_mm = sem("max_mm")
        max_red = sem("max_red")
        max_t = sem("max_t")
        max_hi_s = sem("max_hi_s")
        max_lo_s = sem("max_lo_s")
        max_in = sem("max_in")
        score_mm = sem("score_mm")
        exp_done = sem("exp_done")
        av_done = sem("av_done")
        av_out = sem("av_out")
        y_t = sem("y_t")
        y_rec_s = sem("y_rec_s")
        y_norm = sem("y_norm")
        y_hi_s = sem("y_hi_s")
        y_lo_s = sem("y_lo_s")
        dq_in = sem("dq_in")
        dq_step = sem("dq_step")
        scaled = sem("scaled")
        w_f_s = sem("w_f_s")
        w_hi_s = sem("w_hi_s")
        w_lo_s = sem("w_lo_s")
        acc_in = sem("acc_in")
        gate_mm = sem("gate_mm")
        up_mm = sem("up_mm")
        gelu_s = sem("gelu_s")
        inter_s = sem("inter_s")
        in_hi_s = sem("in_hi_s")
        in_lo_s = sem("in_lo_s")
        down_mm = sem("down_mm")
        sum_mm = sem("sum_mm")
        acc_add = sem("acc_add")
        stored = sem("stored")

        act_spare = nc.scalar.alloc_register("act_spare")
        pool_spare = nc.gpsimd.alloc_register("pool_spare")
        block = ctx.enter_context(nc.Block())

        AHEAD = 10
        PLAN = (
            "A2 m A3 m AO m F1 S0a S1a V1a X d0 m m S2a V1b V1h m S3a m Y S0b MT MH XH YN m m ML S1b A0 m "
            "m A1 m S2b m S3b m Q0a m Q0b m Q0h Q0l",
            "A2 m S0a m d1 K0a K0b m ws K0h S1a m S2a m A3 K0l AO m m S3a Y m MT MH ML S0b m S1b m Q1a YN "
            "m Q1b Q1h m S2b Q1l A0 m m A1 m S3b m",
            "S0a d2 K1a m S1a m K1b K1h m S2a m F0 K1l S3a m A2 m d3 A3 MT AO m MH m S0b ML Y m S1b m V0a "
            "YN m S2b m S3b A0 m m A1 m m",
            "S0a m S1a m A2 m m V0b S2a V0h m m A3 m AO S3a m MT m S0b m Y YN MH m ML S1b m S2b A0 m S3b "
            "U m A1 m m wh",
        )
        WORK = ("Q0", "K0", "Q1", "K1", "V0", "V1")

        def plan(g, first, last):
            tile = AHEAD + sum(steps.split().count("m") for steps in PLAN[:g])
            for step in PLAN[g].split():
                if step in ("A2", "A3", "AO", "Y", "YN") and first and g == 0:
                    continue
                if step in ("MT", "MH", "ML") and last and g == QUADS - 1:
                    continue
                if last and (step in ("X", "XH", "F0") or step[0:2] in WORK and step[0:2] != "V1"):
                    continue
                if step == "m":
                    quad, at = 1 + tile // 16, tile % 16
                    tile += 1
                    if not (last and quad >= QUADS):
                        yield step, (quad, at)
                else:
                    yield step, None

        def of_batch(b, g):
            return (b, g) if g < 4 else (b + 1, g - 4)

        def batches(eng, body):
            body(0, True, False)
            with eng.Fori(1, B - 1) as b:
                body(b, False, False)
            body(B - 1, False, True)

        def wait_from(eng, sem, value):
            if not isinstance(value, int) or value > 0:
                eng.wait_ge(sem, value)

        def chunks(eng, body):
            for g in range(GROUPS):
                if g == 0:
                    body(0, 0)
                with eng.Fori(1 if g == 0 else 0, CHUNKS) as t:
                    body(g, t)

        def wait_apart(eng, spare, sem, value):
            eng.wait_ge(sem, value)
            eng.reg_mov(spare, 0)

        def unit_of(w, u):
            return w[:, u] if isinstance(u, int) else w[:, bass.ds(u, 1)].rearrange("p u e w -> p (u e) w")

        def pair(value):
            return float(np.array([value, value], np.float16).view(np.float32)[0])

        def load_x(sp, b):
            sp.dma_start(x_in, x[b].rearrange("(k p) t -> p k t", p=P)).then_inc(x_loaded, 16)

        def load_unit(sp, n, count):
            wait_from(sp, w_f_s, count)
            sp.dma_start(dq_packed[:, :], packed[n]).then_inc(dq_in, 16)
            sp.dma_start(dq_scales[:, :], scales[n].unsqueeze(1).broadcast_to([8, 16, WORDS])).then_inc(dq_in, 16)

        def store_qk(sp, b, u, side):
            sp.wait_ge(qk_lo, 4 * b + 2 * u + side + 1)
            for n in (2 * side, 2 * side + 1):
                sp.dma_start(qk_dram[u, n].rearrange("r h q -> h r q"), parts[:, u, n]).then_inc(qk_out[u], 16)

        def fill_stack(sp, b, u, first):
            sp.wait_ge(qk_out[u], 64 * b + 64)
            if not first:
                sp.wait_ge(score_mm, 32 * (b - 1) + 16 * u + 16)
            heads = slice(u * UNIT_HEADS, (u + 1) * UNIT_HEADS)
            for j in range(2):
                rows = slice(j * 2 * DH, (j + 1) * 2 * DH)
                sp.dma_start(q_stack[rows, heads, :],
                             qk_dram[u, j:j + 1].broadcast_to([2, DH, UNIT_HEADS, T])).then_inc(stack_in[u], 16)
                sp.dma_start(k_stack[rows, heads, :], qk_dram[u, 2:4]).then_inc(stack_in[u], 16)
            sp.dma_start(k_stack[SEED_ROW:SEED_ROW + 3, heads, :],
                         seed_dram[b].unsqueeze(1).broadcast_to([3, UNIT_HEADS, T])).then_inc(stack_in[u], 16)

        def move_max(sp, b, g):
            sp.wait_ge(max_lo_s, 4 * b + g + 1)
            for i in range(2):
                sp.dma_start(q_stack[MAX_ROW + i:MAX_ROW + i + 1, 4 * g:4 * g + 4, :].rearrange(
                    "o h (t q) -> o (h t) q", q=P), max_rows[i][:, :]).then_inc(max_in, 16)

        def weight_f(pool, n):
            pool.wait_ge(dq_step, DQ_STEPS * n + DQ_STEPS)
            pool.wait_ge(scaled, n + 1)
            wait_from(pool, w_lo_s, n)
            nc.gpsimd.tensor_tensor(dq_w[:, :, :], dq_code[:, :].bitcast(f16).rearrange("p (w e) -> p e w", e=2),
                                    dq_scales[:, :].unsqueeze(1).broadcast_to([P, 2, WORDS]),
                                    ALU.mult).then_inc(w_f_s, 1)

        def weight_scale(act, n):
            act.wait_ge(dq_in, 32 * n + 32)
            nc.scalar.activation(dq_scales[:, :], dq_scales[:, :], ACT.Copy,
                                 scale=CODE_SCALE * W_SCALE).then_inc(scaled, 1)

        def weight_lo(pool, n, w, u):
            wait_apart(pool, pool_spare, w_hi_s, n + 1)
            nc.gpsimd.tensor_tensor(unit_of(w[1], u), dq_w[:, :, :], unit_of(w[0], u),
                                    ALU.subtract).then_inc(w_lo_s, 1)

        def weight_hi(act, n, w, u):
            wait_apart(act, act_spare, w_f_s, n + 1)
            nc.scalar.copy(unit_of(w[0], u), dq_w[:, :, :]).then_inc(w_hi_s, 1)

        def decode(dve, n, k):
            done = DQ_STEPS * n
            if k == 0:
                dve.wait_ge(dq_in, 32 * n + 32)
                wait_from(dve, w_f_s, n)
                nc.vector.scalar_tensor_tensor(out=dq_code[:, :], in0=dq_packed[:, :], scalar=12, in1=dq_packed[:, :],
                                               op0=ALU.logical_shift_left, op1=ALU.bitwise_or).then_inc(dq_step, 1)
            elif k == 1:
                dve.wait_ge(dq_step, done + 1)
                nc.vector.tensor_scalar(dq_sign[:, :], dq_code[:, :], 12, 0x80008000, ALU.logical_shift_left,
                                        ALU.bitwise_and).then_inc(dq_step, 1)
            elif k == 2:
                nc.vector.tensor_scalar(dq_mag[:, :], dq_code[:, :], 9, 0x0E000E00, ALU.logical_shift_left,
                                        ALU.bitwise_and).then_inc(dq_step, 1)
            elif k == 3:
                dve.wait_ge(dq_step, done + 3)
                nc.vector.tensor_tensor(dq_code[:, :], dq_sign[:, :], dq_mag[:, :],
                                        ALU.bitwise_or).then_inc(dq_step, 1)

        @block.sync
        def _(sp):
            load_x(sp, 0)
            for i, w in enumerate((wq, wk, wv)):
                sp.dma_start(w_proj[i], w.rearrange("(k p) o -> p k o", p=P)).then_inc(proj_in[i], 16)
            load_unit(sp, 0, 0)
            sp.wait_ge(setup, 3)
            sp.wait_ge(fixed, 2)
            sp.dma_start(seed_dram, seed).then_inc(seed_out, 16)
            store_qk(sp, 0, 0, 0)
            store_qk(sp, 0, 0, 1)
            sp.wait_ge(seed_out, 16)
            fill_stack(sp, 0, 0, True)
            move_max(sp, 0, 0)

            def body(b, first, last):
                for g in range(QUADS):
                    for step, _ in plan(g, first, last):
                        if step == "ML":
                            move_max(sp, *of_batch(b, g + 1))
                        elif step == "X":
                            sp.wait_ge(x_lo_s, b + 1)
                            if first:
                                sp.wait_ge(v_proj, 1)
                            load_x(sp, b + 1)
                        elif step[0:2] in WORK and step[0] != "V" and step[2] == "l":
                            store_qk(sp, b + 1, int(step[1]), "QK".index(step[0]))
                        elif step == "F0":
                            fill_stack(sp, b + 1, 0, False)
                        elif step == "F1":
                            fill_stack(sp, b, 1, first)
                        elif step == "U":
                            load_unit(sp, b + 1, b + 1)

            batches(sp, body)

            sp.wait_ge(av_done, 8 * B)
            for r in range(CHUNKS):
                sp.dma_start(acc[:, 4 * r:4 * r + 4, :],
                             x.rearrange("b (k p) t -> p (b k) t", p=P)[:, 4 * r:4 * r + 4, :]).then_inc(acc_in, 16)
            with sp.Fori(UNITS + 1, GROUPS * UNITS) as n:
                load_unit(sp, n, n)
            for r in range(4 * CHUNKS):
                sp.wait_ge(acc_add, 4 * (GROUPS - 1) * CHUNKS + r + 1)
                sp.dma_start(out[r * P:(r + 1) * P, :], acc[:, r, :]).then_inc(stored, 16)
            sp.wait_ge(stored, 16 * 4 * CHUNKS)

        @block.gpsimd
        def _(pool):
            nc.gpsimd.memset(k_stack[SEED_ROW:MAX_ROW, :, :].bitcast(f32), 0.0).then_inc(fixed, 1)
            pool.wait_ge(fixed, 1)
            nc.gpsimd.memset(k_stack[MAX_ROW:STACK_ROWS, :, :].bitcast(f32), pair(MAX_K)).then_inc(fixed, 1)
            pool.wait_ge(fixed, 2)
            nc.gpsimd.memset(v_rows[:, :, :, :], 0.0).then_inc(fixed, 1)
            pool.wait_ge(fixed, 3)
            nc.gpsimd.memset(v_rows[:, :, :, DH:DH + 1], 1.0 / Y_SCALE).then_inc(fixed, 1)
            pool.wait_ge(fixed, 4)
            nc.gpsimd.memset(ident[:, :], 0.0).then_inc(ident_in, 1)
            pool.wait_ge(ident_in, 1)
            nc.gpsimd.affine_select(out=ident[:, :], in_=ident[:, :], compare_op=ALU.not_equal, fill=1.0, base=0,
                                    pattern=[[-1, P]], channel_multiplier=1).then_inc(ident_in, 1)

            def split_y(b, g):
                q = 4 * b + g
                cols = bass.ds(b * C + g * 64, 64)
                wait_apart(pool, pool_spare, y_norm, q + 1)
                nc.gpsimd.tensor_copy(y_hi[:, :, cols], y_f[:, :, :]).then_inc(y_hi_s, 1)
                wait_apart(pool, pool_spare, y_hi_s, q + 1)
                nc.gpsimd.tensor_tensor(y_lo[:, :, cols], y_f[:, :, :], y_hi[:, :, cols],
                                        ALU.subtract).then_inc(y_lo_s, 1)

            def x_low(b):
                pool.wait_ge(x_hi_s, b + 1)
                nc.gpsimd.tensor_tensor(x_parts[1][:, :, :], x_in, x_parts[0][:, :, :],
                                        ALU.subtract).then_inc(x_lo_s, 1)

            x_low(0)

            def body(b, first, last):
                for g in range(QUADS):
                    for step, _ in plan(g, first, last):
                        if step == "YN":
                            split_y(*((b, g - 1) if g else (b - 1, 3)))
                        elif step == "XH":
                            x_low(b + 1)
                        elif step == "d3":
                            weight_f(pool, b)
                        elif step == "wh":
                            weight_lo(pool, b, weights[0], b)

            batches(pool, body)
            split_y(B - 1, 3)

            for g in range(GROUPS - 1):
                with pool.Fori(0, CHUNKS) as t:
                    for i in range(2):
                        weight_f(pool, (g + 1) * UNITS + 2 * t + i)
                        weight_lo(pool, (g + 1) * UNITS + 2 * t + i, weights[(g + 1) % 2], 2 * t + i)

        @block.scalar
        def _(act):
            def qk_part(b, side, u, first, bank):
                n = 4 * b + 2 * u + side
                if not first:
                    act.wait_ge(qk_out[u], 64 * b)
                    if side == 0 and u == 0:
                        act.wait_ge(any_set, b + 1)
                act.wait_ge(qk_proj, n + 1)
                scale = (1.0 if first else 1.0 / W_SCALE) if side else any_now[:, :]
                nc.scalar.activation(qk[side][u][0], bank, ACT.Copy, scale=scale).then_inc(qk_hi, 1)

            def v_part(b, u, first, scale):
                act.wait_ge(v_proj, 2 * b + u + 1)
                if not first:
                    act.wait_ge(av_done, 8 * (b - 1) + 4 * u + 4)
                nc.scalar.activation(v_rows[:, :, u * UNIT_HEADS:(u + 1) * UNIT_HEADS, 0:DH],
                                     p_misc.rearrange("p (k h d) -> p k h d", k=TT, h=UNIT_HEADS),
                                     ACT.Copy, scale=scale).then_inc(v_ready, 1)

            def x_high(b):
                act.wait_ge(x_loaded, 16 * b + 16)
                wait_from(act, v_proj, 2 * b)
                nc.scalar.copy(x_parts[0][:, :, :], x_in).then_inc(x_hi_s, 1)

            def max_part(b, g, first):
                q = 4 * b + g
                act.wait_ge(max_t, q + 1)
                if not (first and g == 0):
                    act.wait_ge(max_in, 32 * q)
                nc.scalar.activation(max_rows[0][:, :], p_misc[0:16, 0:P], ACT.Copy,
                                     scale=-1.0 / MAX_K).then_inc(max_hi_s, 1)

            act.dma_start(mask_all[:, 0:T], mask[0].partition_broadcast(P)).then_inc(mask_in, 16)
            act.dma_start(mask_b, mask).then_inc(seed_in, 16)
            act.dma_start(bias_b, bias.partition_broadcast(B)).then_inc(seed_in, 16)
            act.dma_start(mask_all[:, T:],
                          mask[1:].rearrange("b t -> (b t)").partition_broadcast(P)).then_inc(masks_in, 16)
            act.wait_ge(any_set, 1)
            for u in range(2):
                for side in range(2):
                    qk_part(0, side, u, True, psum[:, 2 * u + side, :])
            act.wait_ge(fixed, 4)
            v_part(0, 0, True, 1.0)
            x_high(0)
            for i in range(3):
                act.wait_ge(proj_in[i], 16)
                nc.scalar.activation(w_parts[i][0], w_proj[i], ACT.Copy, scale=W_SCALE).then_inc(wp_hi_s, 1)
            store_qk(act, 0, 1, 0)
            store_qk(act, 0, 1, 1)
            max_part(0, 0, True)

            def body(b, first, last):
                for g in range(QUADS):
                    q = 4 * b + g
                    for step, arg in plan(g, first, last):
                        if step[0] == "S":
                            h, a = int(step[1]), "ab".index(step[2])
                            act.wait_ge(score_mm, 8 * q + 4 * a + h + 1)
                            wait_from(act, av_done, 2 * q - 1 + a)
                            nc.scalar.activation(p_exp[:, a, h], p_score[:, 2 * (h % 2):2 * (h % 2) + 2, :], ACT.Exp,
                                                 scale=SCORE_SCALE).then_inc(exp_done, 1)
                        elif step == "AO":
                            copy_av(q - 1)
                        elif step == "MH":
                            max_part(*of_batch(b, g + 1), False)
                        elif step[0:2] in WORK and step[2] == "h":
                            u = int(step[1])
                            if step[0] == "V":
                                v_part(b + 1 - u, u, first and u == 1, 1.0 / W_SCALE)
                            else:
                                qk_part(b + 1, "QK".index(step[0]), u, False, p_misc)
                        elif step == "XH":
                            x_high(b + 1)
                        elif step == "ws":
                            weight_scale(act, b)
                        elif step == "wh":
                            weight_hi(act, b, weights[0], b)

            def copy_av(q):
                act.wait_ge(av_done, 2 * q + 2)
                wait_from(act, y_t, q)
                nc.scalar.copy(av_sb[:, :], p_av).then_inc(av_out, 1)

            batches(act, body)
            copy_av(4 * B - 1)

            def chunk(g, t):
                for i in range(UNITS):
                    s = (g * CHUNKS + t) * UNITS + i
                    act.wait_ge(gate_mm, s + 1)
                    wait_from(act, inter_s, s - 1)
                    nc.scalar.activation(gelu[:, i % 2, :], p_gate[i % 2], ACT.Gelu_apprx_tanh,
                                         scale=1.0 / (Y_SCALE * W_SCALE)).then_inc(gelu_s, 1)
                    act.wait_ge(inter_s, s + 1)
                    c = g * CHUNKS + t
                    if i >= 2:
                        act.wait_ge(down_mm, (UNITS - 1) * c + i - 1)
                    elif i == 0:
                        wait_from(act, down_mm, (UNITS - 1) * c)
                    else:
                        wait_from(act, sum_mm, 4 * c)
                    nc.scalar.copy(in_hi[:, i % 2, :], inter[:, i % 2, :]).then_inc(in_hi_s, 1)
                    if g < GROUPS - 1 and i % 4 == 0:
                        weight_scale(act, (g + 1) * UNITS + 2 * t + i // 4)
                    if g < GROUPS - 1 and i % 4 == 3:
                        u = 2 * t + i // 4
                        weight_hi(act, (g + 1) * UNITS + u, weights[(g + 1) % 2], u)

            chunks(act, chunk)

        @block.vector
        def _(dve):
            nc.vector.memset(q_stack[SEED_ROW:MAX_ROW, :, :].bitcast(f32), pair(SEED_Q)).then_inc(setup, 1)
            dve.wait_ge(mask_in, 16)
            nc.vector.reduce_max(any_now[:, :], mask_all[:, 0:T], AX.X).then_inc(any_set, 1)
            dve.wait_ge(seed_in, 32)
            nc.vector.reduce_max(any_b, mask_b, AX.X).then_inc(dve_own, 1)
            nc.vector.tensor_scalar(mask_s, mask_b, 1.0, MASK_K, ALU.subtract, ALU.mult).then_inc(dve_own, 1)
            nc.vector.tensor_scalar(bias_s, bias_b, 1.0 / (SCORE_SCALE * SEED_Q), None, ALU.mult).then_inc(dve_own, 1)
            dve.wait_ge(dve_own, 3)
            nc.vector.tensor_scalar(seed[:, 0, :], mask_s, any_b, None, ALU.mult).then_inc(dve_own, 1)
            nc.vector.tensor_scalar(bias_s, bias_s, any_b, None, ALU.mult).then_inc(dve_own, 1)
            dve.wait_ge(dve_own, 5)
            nc.vector.tensor_copy(bias_hi, bias_s).then_inc(dve_own, 1)
            dve.wait_ge(dve_own, 6)
            nc.vector.tensor_tensor(bias_lo, bias_s, bias_hi, ALU.subtract).then_inc(dve_own, 1)
            nc.vector.tensor_scalar(mask_s, mask_b, 0.0, None, ALU.mult).then_inc(dve_own, 1)
            dve.wait_ge(dve_own, 8)
            nc.vector.tensor_scalar(seed[:, 1, :], mask_s, bias_hi, None, ALU.add).then_inc(setup, 1)
            nc.vector.tensor_scalar(seed[:, 2, :], mask_s, bias_lo, None, ALU.add).then_inc(setup, 1)

            def qk_part(b, side, u, bank, first):
                n = 4 * b + 2 * u + side
                dve.wait_ge(qk_hi, n + 1)
                scale = (1.0 if first else 1.0 / W_SCALE) if side else any_now[:, :]
                nc.vector.scalar_tensor_tensor(out=qk[side][u][1], in0=bank, scalar=scale, in1=qk[side][u][0],
                                               op0=ALU.mult, op1=ALU.subtract).then_inc(qk_lo, 1)

            def reduce_maximum(b, g, n):
                q = 4 * b + g
                if n == 0:
                    wait_from(dve, max_t, q - 1)
                dve.wait_ge(max_mm, 16 * q + n + 1)
                nc.vector.reduce_max(maxima[:, g % 2, n:n + 1], p_max[:, n % 2, :], AX.X).then_inc(max_red, 1)

            def max_part(b, g):
                q = 4 * b + g
                dve.wait_ge(max_hi_s, q + 1)
                nc.vector.scalar_tensor_tensor(out=max_rows[1][:, :], in0=p_misc[0:16, 0:P], scalar=-1.0 / MAX_K,
                                               in1=max_rows[0][:, :], op0=ALU.mult,
                                               op1=ALU.subtract).then_inc(max_lo_s, 1)

            def normalise(q):
                dve.wait_ge(y_t, q + 1)
                nc.vector.reciprocal(y_rec[:, :, :], y_rows[:, :, :, DH]).then_inc(y_rec_s, 1)
                dve.wait_ge(y_rec_s, q + 1)
                wait_from(dve, y_lo_s, q)
                nc.vector.tensor_tensor(y_f[:, :, :].rearrange("p k (h d) -> p k h d", h=4), y_rows[:, :, :, 0:DH],
                                        y_rec[:, :, :].unsqueeze(3).broadcast_to([P, TT, 4, DH]),
                                        ALU.mult).then_inc(y_norm, 1)

            y_rows = p_av.rearrange("p (k h d) -> p k h d", k=TT, h=4)
            for side, u in ((0, 0), (1, 0), (0, 1), (1, 1)):
                qk_part(0, side, u, psum[:, 2 * u + side, :], True)
            dve.wait_ge(masks_in, 16)
            nc.vector.reduce_max(any_key[:, :], mask_all.rearrange("p (b t) -> p b t", b=B),
                                 AX.X).then_inc(dve_own, 1)
            for i in range(3):
                dve.wait_ge(wp_hi_s, i + 1)
                nc.vector.scalar_tensor_tensor(out=w_parts[i][1], in0=w_proj[i], scalar=W_SCALE, in1=w_parts[i][0],
                                               op0=ALU.mult, op1=ALU.subtract).then_inc(wp_lo_s, 1)
            dve.wait_ge(dve_own, 9)
            nc.vector.tensor_scalar(any_key[:, :], any_key[:, :], 1.0 / W_SCALE, None, ALU.mult).then_inc(dve_own, 1)
            dve.wait_ge(dve_own, 10)
            for n in range(16):
                reduce_maximum(0, 0, n)
            max_part(0, 0)
            for n in range(AHEAD):
                reduce_maximum(0, 1, n)

            def body(b, first, last):
                if not last:
                    nc.vector.tensor_copy(any_now[:, :], any_key[:, bass.ds(b + 1, 1)]).then_inc(any_set, 1)
                for g in range(QUADS):
                    for step, arg in plan(g, first, last):
                        if step == "m":
                            reduce_maximum(*of_batch(b, arg[0]), arg[1])
                        elif step == "ML":
                            max_part(*of_batch(b, g + 1))
                        elif step == "YN":
                            normalise(4 * b + g - 1)
                        elif step[0:2] in WORK and step[2] == "l":
                            qk_part(b + 1, "QK".index(step[0]), int(step[1]), p_misc, False)
                        elif step[0] == "d":
                            decode(dve, b, int(step[1]))

            batches(dve, body)
            normalise(4 * B - 1)

            def chunk(g, t):
                for i in range(UNITS):
                    s = (g * CHUNKS + t) * UNITS + i
                    dve.wait_ge(gelu_s, s + 1)
                    dve.wait_ge(up_mm, s + 1)
                    wait_from(dve, in_lo_s, s - 1)
                    nc.vector.scalar_tensor_tensor(out=inter[:, i % 2, :], in0=p_up[i % 2],
                                                   scalar=I_SCALE / (Y_SCALE * W_SCALE), in1=gelu[:, i % 2, :],
                                                   op0=ALU.mult, op1=ALU.mult).then_inc(inter_s, 1)
                    dve.wait_ge(in_hi_s, s + 1)
                    nc.vector.tensor_tensor(in_lo[:, i % 2, :], inter[:, i % 2, :], in_hi[:, i % 2, :],
                                            ALU.subtract).then_inc(in_lo_s, 1)
                    if g < GROUPS - 1:
                        for k in ((0,), (1, 2), (3,), ())[i % 4]:
                            decode(dve, (g + 1) * UNITS + 2 * t + i // 4, k)
                c = g * CHUNKS + t
                for r in range(4):
                    dve.wait_ge(sum_mm, 4 * c + r + 1)
                    if g == 0:
                        dve.wait_ge(acc_in, 16 * CHUNKS)
                    rows = acc[:, bass.ds(4 * t + r, 1), :].rearrange("p r h -> p (r h)")
                    if g > 0:
                        dve.wait_ge(acc_add, 4 * (c - CHUNKS) + r + 1)
                    nc.vector.scalar_tensor_tensor(out=rows, in0=p_out[r], scalar=1.0 / (I_SCALE * W_SCALE),
                                                   in1=rows, op0=ALU.mult, op1=ALU.add).then_inc(acc_add, 1)

            chunks(dve, chunk)

        @block.tensor
        def _(pe):
            def first_qk(side, u, bank):
                for k in range(CK):
                    last = nc.tensor.matmul(bank, w_proj[side][:, k, u * P:(u + 1) * P], x_in[:, k, :],
                                            start=(k == 0), stop=(k == CK - 1))
                last.then_inc(qk_proj, 1)

            def first_v():
                for t in range(TT):
                    for k in range(CK):
                        last = nc.tensor.matmul(p_misc[:, t * P:(t + 1) * P], x_in[:, k, t * P:(t + 1) * P],
                                                w_proj[2][:, k, 0:P], start=(k == 0), stop=(k == CK - 1))
                last.then_inc(v_proj, 1)

            def project_qk(side, u, k):
                for n, (i, j) in enumerate(((0, 0), (0, 1), (1, 0))):
                    last = nc.tensor.matmul(p_misc, w_parts[side][i][:, k, u * P:(u + 1) * P], x_parts[j][:, k, :],
                                            start=(k == 0 and n == 0), stop=(k == CK - 1 and n == 2))
                if k == CK - 1:
                    last.then_inc(qk_proj, 1)

            def project_v(u, i):
                for t in (2 * i, 2 * i + 1):
                    for k in range(CK):
                        for n, (a, c) in enumerate(((0, 0), (0, 1), (1, 0))):
                            last = nc.tensor.matmul(p_misc[:, t * P:(t + 1) * P], x_parts[a][:, k, t * P:(t + 1) * P],
                                                    w_parts[2][c][:, k, u * P:(u + 1) * P],
                                                    start=(k == 0 and n == 0), stop=(k == CK - 1 and n == 2))
                if i == 1:
                    last.then_inc(v_proj, 1)

            def max_tile(b, g, n):
                if n == 0:
                    pe.wait_ge(stack_in[g // 2], 16 * STACK_DMAS * b + 16 * STACK_DMAS)
                wait_from(pe, max_red, 16 * (4 * b + g) + n - 1)
                h, t = 4 * g + n // 4, n % 4
                nc.tensor.matmul(p_max[:, n % 2, :], q_stack[0:MAX_ROW, h, t * P:(t + 1) * P],
                                 k_stack[0:MAX_ROW, h, :], start=True, stop=True).then_inc(max_mm, 1)

            def transpose_maxima(b, g):
                pe.wait_ge(max_red, 16 * (4 * b + g) + 16)
                nc.tensor.transpose(p_misc[0:16, 0:P], maxima[:, g % 2, :], ident[:, :]).then_inc(max_t, 1)

            def scores(b, g, h, a):
                n = 8 * (4 * b + g) + 4 * a + h
                if h == 0 and a == 0:
                    pe.wait_ge(max_in, 32 * (4 * b + g) + 32)
                wait_from(pe, exp_done, n - 1)
                for j in range(2):
                    k = 2 * a + j
                    last = nc.tensor.matmul(p_score[:, 2 * (h % 2) + j, :],
                                            k_stack[0:STACK_ROWS, 4 * g + h, k * P:(k + 1) * P],
                                            q_stack[0:STACK_ROWS, 4 * g + h, :], start=True, stop=True)
                last.then_inc(score_mm, 1)

            def product_v(b, g, k):
                q, a, j = 4 * b + g, k // 2, k % 2
                if j == 0:
                    pe.wait_ge(exp_done, 8 * q + 4 * a + 4)
                if k == 0:
                    pe.wait_ge(v_ready, 2 * b + g // 2 + 1)
                    wait_from(pe, y_norm, q)
                for h in range(4):
                    last = nc.tensor.matmul(p_av[32 * h:32 * h + 32, :], v_rows[:, k, 4 * g + h, :],
                                            p_exp[:, a, h, j, :], start=(k == 0), stop=(k == TT - 1))
                if j == 1:
                    last.then_inc(av_done, 1)

            def transpose_y(q):
                pe.wait_ge(av_out, q + 1)
                for t in range(TT):
                    last = nc.tensor.transpose(p_av[:, t * P:(t + 1) * P], av_sb[:, t * P:(t + 1) * P], ident[:, :])
                last.then_inc(y_t, 1)

            pe.wait_ge(x_loaded, 16)
            for u in range(2):
                for side in range(2):
                    pe.wait_ge(proj_in[side], 16)
                    first_qk(side, u, psum[:, 2 * u + side, :])
            pe.wait_ge(proj_in[2], 16)
            first_v()
            for n in range(16):
                max_tile(0, 0, n)
            pe.wait_ge(v_ready, 1)
            pe.wait_ge(ident_in, 2)
            transpose_maxima(0, 0)
            for n in range(AHEAD):
                max_tile(0, 1, n)

            def three_products(dst, w, cols, i, t, tiles=range(TT)):
                rows = bass.ds(t * 512, 512)
                for k in tiles:
                    c = slice(cols + k // 2 * P, cols + k // 2 * P + P)
                    nc.tensor.matmul(dst, w[0][:, i, k % 2, c], y_hi[:, k, rows], start=(k == 0), stop=False)
                    nc.tensor.matmul(dst, w[0][:, i, k % 2, c], y_lo[:, k, rows], start=False, stop=False)
                    last = nc.tensor.matmul(dst, w[1][:, i, k % 2, c], y_hi[:, k, rows], start=False,
                                            stop=(k == TT - 1))
                return last

            def first_gate_up(n):
                if n == 0:
                    pe.wait_ge(max_red, 16 * 4 * B)
                    pe.wait_ge(y_lo_s, 8)
                    pe.wait_ge(w_lo_s, 1)
                dst = (p_gate, p_up)[n // TT][0]
                done = three_products(dst, weights[0], 2 * P * (n // TT), 0, 0, (n % TT,))
                if n % TT == TT - 1:
                    done.then_inc((gate_mm, up_mm)[n // TT], 1)

            def body(b, first, last):
                misc = (max_lo_s, 4 * b + 1)
                for g in range(QUADS):
                    q = 4 * b + g
                    for step, arg in plan(g, first, last):
                        if step[0] == "S":
                            scores(b, g, int(step[1]), "ab".index(step[2]))
                            if last and g == QUADS - 1:
                                first_gate_up(4 * "ab".index(step[2]) + int(step[1]))
                        elif step == "m":
                            max_tile(*of_batch(b, arg[0]), arg[1])
                        elif step in ("A2", "A3"):
                            product_v(*((b, g - 1) if g else (b - 1, 3)), int(step[1]))
                        elif step in ("A0", "A1"):
                            product_v(b, g, int(step[1]))
                        elif step == "Y":
                            transpose_y(q - 1)
                        elif step == "MT":
                            pe.wait_ge(*misc)
                            transpose_maxima(*of_batch(b, g + 1))
                            misc = (max_lo_s, q + 2)
                        elif step[0:2] in WORK and step[2] in "ab":
                            u, piece = int(step[1]), "ab".index(step[2])
                            if piece == 0:
                                pe.wait_ge(*misc)
                            if step == "V1a":
                                pe.wait_ge(wp_lo_s, 3)
                                pe.wait_ge(x_lo_s, b + 1)
                            if step == "Q0a":
                                pe.wait_ge(x_lo_s, b + 2)
                            if step[0] == "V":
                                project_v(u, piece)
                                misc = (v_ready, 2 * (b + 1 - u) + u + 1)
                            else:
                                side = "QK".index(step[0])
                                project_qk(side, u, piece)
                                misc = (qk_lo, 4 * (b + 1) + 2 * u + side + 1)

            batches(pe, body)
            product_v(B - 1, 3, 2)
            product_v(B - 1, 3, 3)

            def down(g, t, i, w):
                s = (g * CHUNKS + t) * UNITS + i
                pe.wait_ge(in_lo_s, s + 1)
                e, u = i % 2, i - i % 2
                w_hi, w_lo = (w[p][:, u:u + 2, e, 4 * P:4 * P + 256] for p in range(2))
                for r in range(4):
                    dst = p_out[r]
                    if i == 0:
                        wait_from(pe, acc_add, 4 * (g * CHUNKS + t) - 3 + r)
                    rows = slice(r * P, (r + 1) * P)
                    nc.tensor.matmul(dst, in_hi[:, i % 2, rows], w_hi, start=(i == 0), stop=False)
                    nc.tensor.matmul(dst, in_hi[:, i % 2, rows], w_lo, start=False, stop=False)
                    last = nc.tensor.matmul(dst, in_lo[:, i % 2, rows], w_hi, start=False, stop=(i == UNITS - 1))
                    if i == UNITS - 1:
                        last.then_inc(sum_mm, 1)
                if i < UNITS - 1:
                    last.then_inc(down_mm, 1)

            def chunk(g, t):
                w = weights[g % 2]
                start = isinstance(t, int) and g == t == 0
                if start:
                    pe.wait_ge(exp_done, 32 * B)
                else:
                    if g == 0:
                        pe.wait_ge(y_lo_s, 8 * t + 8)
                    pe.wait_ge(w_lo_s, UNITS * (g + 1))
                for i in range(UNITS):
                    s = (g * CHUNKS + t) * UNITS + i
                    if start and i == 0:
                        continue
                    if start:
                        pe.wait_ge(w_lo_s, i + 1)
                    wait_from(pe, gelu_s, s - 1)
                    three_products(p_gate[i % 2], w, 0, i, t).then_inc(gate_mm, 1)
                    if start and i == 1:
                        transpose_y(4 * B - 1)
                    wait_from(pe, inter_s, s - 1)
                    three_products(p_up[i % 2], w, 2 * P, i, t).then_inc(up_mm, 1)
                    if start and i == 1:
                        pe.wait_ge(y_norm, 4 * B)
                    if i:
                        down(g, t, i - 1, w)
                down(g, t, UNITS - 1, w)

            chunks(pe, chunk)


def by_parity(a, axis):
    shape = a.shape
    a = a.reshape(*shape[:axis], shape[axis] // 256, 128, 2, *shape[axis + 1:])
    return a.swapaxes(axis + 1, axis + 2).reshape(shape)


def kernel(**inputs):
    import concourse.bacc as bacc
    import numpy as np
    from concourse.bass_utils import run_bass_kernel_spmd

    given = {k: np.asarray(v) for k, v in inputs.items()}

    def ffn_units(gate, up, down):
        r = gate.shape[0] // 2
        g, u = (a.reshape(2, r, F // P, P).transpose(2, 1, 0, 3).reshape(F // P, r, 2 * P) for a in (gate, up))
        d = down.reshape(F // 256, r, 2, 256).transpose(0, 2, 1, 3).reshape(F // P, r, 256)
        return np.ascontiguousarray(np.concatenate([g, u, d], axis=2))

    gate_w, up_w = (by_parity(given[f"L0_ffn_{n}_W_packed"], 0).T for n in ("gate", "up"))
    gate_s, up_s = (by_parity(given[f"L0_ffn_{n}_scales"], 0).T for n in ("gate", "up"))
    down_w, down_s = (by_parity(given[f"L0_ffn_down_{n}"], 0).T for n in ("W_packed", "scales"))
    arrays = {
        "x": by_parity(given["x"], 2),
        "mask": by_parity(given["cond_2048"], 1),
        "bias": given["L0_cond_b"],
        "wq": given["L0_cond_Wq"].T,
        "wk": given["L0_cond_Wk"].T,
        "wv": given["L0_cond_Wv"].T,
        "packed": ffn_units(gate_w, up_w, down_w).view(np.uint32),
        "scales": ffn_units(gate_s, up_s, down_s),
    }
    arrays = {k: np.ascontiguousarray(v) for k, v in arrays.items()}
    nc = bacc.Bacc("TRN2", target_bir_lowering=False, num_devices=1)
    args = {k: nc.dram_tensor(k, v.shape, mybir.dt.from_np(v.dtype), kind="ExternalInput").ap()
            for k, v in arrays.items()}
    out = nc.dram_tensor("out", (B * C, T), mybir.dt.float32, kind="ExternalOutput").ap()
    build(nc, out=out, **args)
    r = run_bass_kernel_spmd(nc, [arrays], core_ids=[0])
    got = r.results[0]["out"].reshape(B, C, T // 256, 2, 128)
    return np.ascontiguousarray(got.swapaxes(3, 4)).reshape(B, C, T)
```
